# Optimizing a Trainium2 kernel written in Bass

```python
import numpy as np
import jax
import jax.numpy as jnp

def _softmax(x, axis=-1):
    return jax.nn.softmax(x, axis=axis)

def _gelu(x):
    return jax.nn.gelu(x, approximate=True)

def _silu(x):
    return jax.nn.silu(x)

def _sigmoid(x):
    return jax.nn.sigmoid(x)

def _layernorm(x, axis=-1, eps=1e-05):
    m = jnp.mean(x, axis=axis, keepdims=True)
    v = jnp.var(x, axis=axis, keepdims=True)
    return (x - m) / jnp.sqrt(v + eps)

def _scatter_add(tgt, idx, src, axis=0):
    return tgt.at[idx].add(src)

def _segment_sum(src, seg, n):
    return jax.ops.segment_sum(src, seg, n)
kernel_name = 'mk_macaron_d1_jaxref_r4_d4a4eb'

def setup_inputs(seed: int=0):
    np.random.seed(seed)
    _w = jnp.asarray

    def _L0_attn_setup():
        import jax, jax.numpy as jnp
        import numpy as np
        D_MODEL = 256
        D_STATE = 16
        D_CONV = 4
        EXPAND = 2
        D_INNER = D_MODEL * EXPAND

        def soft_clamp(x, lo, hi, sharp):
            c = (hi + lo) / 2.0
            r = (hi - lo) / 2.0
            return jnp.tanh((x - c) / (r + 1e-08) * sharp) / sharp * r + c
        key = jax.random.key(seed)
        ks = jax.random.split(key, 9)
        B, L = (2, 256)
        x = jax.random.normal(ks[0], (B, L, D_MODEL), jnp.float32)
        norm_w = jnp.ones((D_MODEL,), jnp.float32)
        W_in = jax.random.normal(ks[1], (2 * D_INNER, D_MODEL), jnp.float32) * 0.02
        conv_w = jax.random.normal(ks[2], (D_INNER, 1, D_CONV), jnp.float32) * 0.02
        conv_b = jnp.zeros((D_INNER,), jnp.float32)
        W_dt = jax.random.normal(ks[3], (D_INNER, D_INNER), jnp.float32) * 0.02
        b_dt = jnp.full((D_INNER,), -2.0, jnp.float32)
        W_B = jax.random.normal(ks[4], (D_STATE, D_INNER), jnp.float32) * 0.02
        W_C = jax.random.normal(ks[5], (D_STATE, D_INNER), jnp.float32) * 0.02
        A_log = jax.random.normal(ks[6], (D_INNER, D_STATE), jnp.float32) * 0.1
        D_param = jnp.full((D_INNER,), 0.1, jnp.float32)
        W_out = jax.random.normal(ks[7], (D_MODEL, D_INNER), jnp.float32) * 0.02
        residual_scale = jnp.asarray(0.3, jnp.float32)
        return dict(x=x, norm_w=norm_w, W_in=W_in, conv_w=conv_w, conv_b=conv_b, W_dt=W_dt, b_dt=b_dt, W_B=W_B, W_C=W_C, A_log=A_log, D_param=D_param, W_out=W_out, residual_scale=residual_scale)
    _L0_attn_in = _L0_attn_setup()

    def _L0_ffn_setup():
        import jax, jax.numpy as jnp
        import numpy as np

        def _binarize(w):
            alpha = jax.lax.stop_gradient(jnp.mean(jnp.abs(w), axis=1, keepdims=True))
            bw = alpha * jnp.sign(w)
            return w + jax.lax.stop_gradient(bw - w)
        key = jax.random.key(seed)
        k1, k2, k3, k4, k5 = jax.random.split(key, 5)
        D, H = (256, 1024)
        x = jax.random.normal(k1, (64, 196, D), dtype=jnp.float32)
        w1 = jax.random.normal(k2, (H, D), dtype=jnp.float32) * 0.02
        b1 = jax.random.normal(k3, (H,), dtype=jnp.float32) * 0.02
        w2 = jax.random.normal(k4, (D, H), dtype=jnp.float32) * 0.02
        b2 = jax.random.normal(k5, (D,), dtype=jnp.float32) * 0.02
        return {'x': x, 'w1': w1, 'b1': b1, 'w2': w2, 'b2': b2}
    _L0_ffn_in = _L0_ffn_setup()
    _d = {'L0_attn_x': _L0_attn_in['x'], 'L0_attn_norm_w': _L0_attn_in['norm_w'], 'L0_attn_W_in': _L0_attn_in['W_in'], 'L0_attn_conv_w': _L0_attn_in['conv_w'], 'L0_attn_conv_b': _L0_attn_in['conv_b'], 'L0_attn_W_dt': _L0_attn_in['W_dt'], 'L0_attn_b_dt': _L0_attn_in['b_dt'], 'L0_attn_W_B': _L0_attn_in['W_B'], 'L0_attn_W_C': _L0_attn_in['W_C'], 'L0_attn_A_log': _L0_attn_in['A_log'], 'L0_attn_D_param': _L0_attn_in['D_param'], 'L0_attn_W_out': _L0_attn_in['W_out'], 'L0_attn_residual_scale': _L0_attn_in['residual_scale'], 'L0_ffn_w1': _L0_ffn_in['w1'], 'L0_ffn_b1': _L0_ffn_in['b1'], 'L0_ffn_w2': _L0_ffn_in['w2'], 'L0_ffn_b2': _L0_ffn_in['b2']}
    _x0 = _d['L0_attn_x']
    _d['L0_attn_x'] = jax.random.normal(jax.random.fold_in(jax.random.key(seed), 1), (2, 2048, 256), dtype=_x0.dtype)
    del _x0
    return _d

def reference(L0_attn_x, L0_attn_norm_w, L0_attn_W_in, L0_attn_conv_w, L0_attn_conv_b, L0_attn_W_dt, L0_attn_b_dt, L0_attn_W_B, L0_attn_W_C, L0_attn_A_log, L0_attn_D_param, L0_attn_W_out, L0_attn_residual_scale, L0_ffn_w1, L0_ffn_b1, L0_ffn_w2, L0_ffn_b2):

    def _L0_attn_ref(x, norm_w, W_in, conv_w, conv_b, W_dt, b_dt, W_B, W_C, A_log, D_param, W_out, residual_scale):
        import jax, jax.numpy as jnp
        import numpy as np
        D_MODEL = 256
        D_STATE = 16
        D_CONV = 4
        EXPAND = 2
        D_INNER = D_MODEL * EXPAND

        def soft_clamp(x, lo, hi, sharp):
            c = (hi + lo) / 2.0
            r = (hi - lo) / 2.0
            return jnp.tanh((x - c) / (r + 1e-08) * sharp) / sharp * r + c
        B, L, _ = x.shape
        var = jnp.mean(x * x, axis=-1, keepdims=True)
        xn = x * jax.lax.rsqrt(var + 1e-06) * norm_w
        proj = xn @ W_in.T
        x_branch, gate = (proj[..., :D_INNER], proj[..., D_INNER:])
        xc = jax.lax.conv_general_dilated(jnp.swapaxes(x_branch, 1, 2), conv_w, (1,), [(D_CONV - 1, 0)], dimension_numbers=('NCH', 'OIH', 'NCH'), feature_group_count=D_INNER)
        xc = xc + conv_b[None, :, None]
        xc = jnp.swapaxes(xc, 1, 2)
        xc = xc * jax.nn.sigmoid(xc)
        dt = soft_clamp(jax.nn.softplus(xc @ W_dt.T + b_dt), 0.001, 0.1, 0.5)
        Bp = xc @ W_B.T
        Cp = xc @ W_C.T
        A = -jnp.exp(soft_clamp(A_log, -5.0, 5.0, 0.5))
        dt_A = soft_clamp(dt[..., None] * A[None, None], -8.0, 8.0, 0.5)
        dA = jnp.exp(dt_A)
        dB = dt[..., None] * Bp[:, :, None, :]
        h0 = jnp.zeros((B, D_INNER, D_STATE), jnp.float32)

        def step(h, inp):
            dA_t, dB_t, x_t, C_t, t = inp
            h = h * dA_t + dB_t * x_t[:, :, None]
            nrm = jnp.sqrt(jnp.sum(h * h, axis=(1, 2), keepdims=True))
            fac = jnp.minimum(20.0 / (nrm + 1e-08), 1.0)
            h = jnp.where(t % 10 == 0, h * fac, h)
            y = jnp.einsum('bdn,bn->bd', h, C_t) + D_param * x_t
            return (h, y)
        xs = (jnp.swapaxes(dA, 0, 1), jnp.swapaxes(dB, 0, 1), jnp.swapaxes(xc, 0, 1), jnp.swapaxes(Cp, 0, 1), jnp.arange(L))
        _, ys = jax.lax.scan(step, h0, xs)
        x_ssm = jnp.swapaxes(ys, 0, 1)
        x_out = x_ssm * (gate * jax.nn.sigmoid(gate)) @ W_out.T
        scale = jax.nn.sigmoid(residual_scale) * 0.5
        return x + scale * x_out

    def _L0_ffn_ref(x, w1, b1, w2, b2):
        import jax, jax.numpy as jnp
        import numpy as np

        def _binarize(w):
            alpha = jax.lax.stop_gradient(jnp.mean(jnp.abs(w), axis=1, keepdims=True))
            bw = alpha * jnp.sign(w)
            return w + jax.lax.stop_gradient(bw - w)
        bw1 = _binarize(w1)
        h = jnp.einsum('bsd,hd->bsh', x, bw1) + b1
        h = jax.nn.gelu(h, approximate=False)
        bw2 = _binarize(w2)
        out = jnp.einsum('bsh,dh->bsd', h, bw2) + b2
        return out
    x = L0_attn_x
    x = x + 0.5 * _L0_ffn_ref(_layernorm(x, axis=-1), L0_ffn_w1, L0_ffn_b1, L0_ffn_w2, L0_ffn_b2)
    x = x + _L0_attn_ref(_layernorm(x, axis=-1), L0_attn_norm_w, L0_attn_W_in, L0_attn_conv_w, L0_attn_conv_b, L0_attn_W_dt, L0_attn_b_dt, L0_attn_W_B, L0_attn_W_C, L0_attn_A_log, L0_attn_D_param, L0_attn_W_out, L0_attn_residual_scale)
    x = x + 0.5 * _L0_ffn_ref(_layernorm(x, axis=-1), L0_ffn_w1, L0_ffn_b1, L0_ffn_w2, L0_ffn_b2)
    return x

_drawn_inputs = setup_inputs


def setup_inputs(seed=0):
    import zlib

    import numpy as np

    out = dict(_drawn_inputs(seed))
    spreads = {'L0_attn_norm_w': (1.0, 0.6),
     'L0_attn_conv_b': (0.0, 0.8),
     'L0_attn_b_dt': (-2.0, 0.6),
     'L0_attn_D_param': (0.10000000149011612, 0.6)}
    factors = {'L0_attn_W_in': 8.0,
     'L0_attn_conv_w': 8.0,
     'L0_attn_W_dt': 8.0,
     'L0_attn_W_B': 8.0,
     'L0_attn_W_C': 8.0,
     'L0_attn_A_log': 8.0,
     'L0_attn_W_out': 8.0,
     'L0_ffn_b1': 8.0,
     'L0_ffn_b2': 3.88}
    for name, (base, spread) in spreads.items():
        noise = np.random.default_rng([zlib.crc32(name.encode()), seed]).standard_normal(out[name].shape)
        drawn = base * np.exp(spread * noise) if base else spread * noise
        out[name] = jnp.asarray(drawn.astype(out[name].dtype))
    for name, factor in factors.items():
        out[name] = (out[name] * factor).astype(out[name].dtype)
    return out
```

```python
from contextlib import ExitStack

import concourse.bass as bass
from concourse import mybir

F32 = mybir.dt.float32
ALU = mybir.AluOpType
ACT = mybir.ActivationFunctionType

P = 128
B, L, D = 2, 2048, 256
E = 512
N = 16
H = 1024
TAPS = 4
KD, KE, KH = D // P, E // P, H // P
TT = 256
TILES = L // TT
G = B * TT // P
COLS = B * TT

S = 10
W = S + 1
ROWS = KE * B * N
CB = 12
CT = CB * S
BLOCKS = -(-L // S)
PAIRS_BODY = 12
BODY = 2 * CB
TURNS = BLOCKS // BODY
TAIL = -(-(BLOCKS - TURNS * BODY) // 2) * 2
CHUNKS = 2 * TURNS + -(-TAIL // CB)
LP = (CHUNKS * CB + 1) * S + 8
HALF = CT // 2

DT_MID, DT_HALF = (0.1 + 0.001) / 2, (0.1 - 0.001) / 2
A_HALF = 5.0
DTA_HALF = 8.0
SHARP = 0.5


FIRST = 1


def prime(nc, sems):
    engines = (nc.sync, nc.gpsimd, nc.vector, nc.scalar)
    for k, s in enumerate(sems):
        engines[k % 4].sem_inc(s, FIRST)
    nc.all_engine_barrier()


class Chain:

    def __init__(self, eng, sem, per, turn):
        self.eng, self.sem, self.base, self.n, self.per = eng, sem, turn * per + FIRST, 0, per

    def add(self, ins):
        self.n += 1
        ins.then_inc(self.sem, 1)

    def sync(self):
        self.eng.wait_ge(self.sem, self.base + self.n)

    def done(self):
        assert self.n == self.per, (self.n, self.per)


def hold(eng, settled, sem, value):
    if not isinstance(value, int):
        value = eng.to_reg(value)
        eng.wait_ge(*settled)
    eng.wait_ge(sem, value)


class FfnWeights:

    def __init__(self, nc, ctx, dram, tag):
        def sb(name, shape):
            return ctx.enter_context(nc.sbuf_tensor(f"{tag}_{name}", shape, F32))

        def sem(name):
            return ctx.enter_context(nc.semaphore(f"{tag}_{name}"))

        self.dram = dram
        self.s1 = sb("s1", [P, KD, H])
        self.s2 = sb("s2", [P, KH, D])
        self.a1 = sb("a1", [P, KH])
        self.b1 = sb("b1", [P, KH])
        self.a2 = sb("a2", [P, D])
        self.b2 = sb("b2", [P, D])
        self.ident = sb("ident", [P, P])
        self.ones = sb("ones", [P, P])
        self.mhalf = sb("mhalf", [P, G])
        self.loaded = sem("w_loaded")
        self.abs1 = sem("w_abs1")
        self.abs2 = sem("w_abs2")
        self.sum2 = sem("w_sum2")
        self.signs = sem("w_signs")
        self.consts = sem("w_consts")
        self.filled = sem("w_filled")
        self.ready = sem("w_ready")

    def load(self, sp, w1n):
        d = self.dram
        sp.dma_start(w1n[:], d["w1"].rearrange("(m p) k -> p m k", p=P)).then_inc(self.loaded, 16)
        sp.dma_start(self.s1[:], d["w1T"].rearrange("(k p) h -> p k h", p=P)).then_inc(self.loaded, 16)
        sp.dma_start(self.s2[:], d["w2T"].rearrange("(k p) d -> p k d", p=P)).then_inc(self.loaded, 16)
        sp.dma_start(self.b1[:], d["b1"]).then_inc(self.loaded, 16)
        sp.dma_start(self.b2[:], d["b2"].broadcast_to([P, D])).then_inc(self.loaded, 16)

    def on_act(self, act, w1n, w2abs):
        act.wait_ge(self.loaded, 80)
        for m in range(KH):
            act.activation(w1n[:, m, :], w1n[:, m, :], ACT.Abs,
                           accum_out=self.a1[:, m:m + 1]).then_inc(self.abs1, 1)
        act.activation(w2abs[:], self.s2[:], ACT.Abs).then_inc(self.abs2, 1)
        act.activation(self.s1[:], self.s1[:], ACT.Sign).then_inc(self.signs, 1)
        act.wait_ge(self.abs2, 1)
        act.activation(self.s2[:], self.s2[:], ACT.Sign).then_inc(self.signs, 1)

    def on_pool(self, pool):
        pool.memset(self.ident[:], 0.0).then_inc(self.filled, 1)
        pool.memset(self.ones[:], 1.0).then_inc(self.filled, 1)
        pool.memset(self.mhalf[:], -0.5).then_inc(self.filled, 1)
        pool.wait_ge(self.filled, 3)
        pool.affine_select(out=self.ident[:], in_=self.ident[:], compare_op=ALU.not_equal, fill=1.0,
                           base=0, pattern=[[-1, P]], channel_multiplier=1).then_inc(self.consts, 1)

    def on_pe(self, pe, w2abs, psum):
        pe.wait_ge(self.consts, 1)
        pe.wait_ge(self.abs2, 1)
        for k in range(KH):
            mm = pe.matmul(psum, self.ones[:], w2abs[:, k, :], start=(k == 0), stop=(k == KH - 1))
        mm.then_inc(self.sum2, 1)

    def on_dve(self, dve, psum):
        dve.wait_ge(self.abs1, KH)
        dve.wait_ge(self.loaded, 80)
        dve.tensor_scalar(self.a1[:], self.a1[:], 1.0 / D, None, ALU.mult).then_inc(self.ready, 1)
        dve.tensor_scalar(self.b2[:], self.b2[:], 0.5, None, ALU.mult).then_inc(self.ready, 1)
        dve.wait_ge(self.sum2, 1)
        dve.tensor_scalar(self.a2[:], psum, 0.5 / H, None, ALU.mult).then_inc(self.ready, 1)
        dve.wait_ge(self.ready, 3)


class RowNorm:

    STEPS = 3 * G + 1 - G

    def __init__(self, nc, ctx, tag, eps, mhalf, consts):
        self.st = ctx.enter_context(nc.sbuf_tensor(f"{tag}_st", [P, G, 6], F32))
        self.mv = ctx.enter_context(nc.sbuf_tensor(f"{tag}_mv", [P, G, 2], F32))
        self.ve = ctx.enter_context(nc.sbuf_tensor(f"{tag}_ve", [P, G], F32))
        self.rs = ctx.enter_context(nc.sbuf_tensor(f"{tag}_rs", [P, G], F32))
        self.var_ready = ctx.enter_context(nc.semaphore(f"{tag}_var_ready"))
        self.rstd_ready = ctx.enter_context(nc.semaphore(f"{tag}_rstd_ready"))
        self.eps, self.mhalf, self.consts = eps, mhalf, consts

    def stats(self, dve, ch, src, i):
        for g in range(G):
            ch.add(dve.bn_stats(self.st[:, g, :], src[:, g, :]))
        hold(dve, (self.consts, 1), ch.sem, ch.base + ch.n)
        for g in range(G):
            ch.add(dve.bn_aggr(self.mv[:, g, :], self.st[:, g, :]))
        ch.sync()
        dve.tensor_scalar(self.ve[:], self.mv[:, :, 1], self.eps, None, ALU.add).then_inc(self.var_ready, 1)

    def on_pool(self, pool, i):
        pool.wait_ge(self.var_ready, i + 1)
        pool.tensor_tensor(self.rs[:], self.ve[:], self.mhalf, ALU.pow).then_inc(self.rstd_ready, 1)

    def apply(self, dve, src, dst, i, done):
        dve.wait_ge(self.rstd_ready, i + 1)
        for g in range(G):
            dve.tensor_scalar(dst[:, g, :], src[:, g, :], self.mv[:, g, 0:1], self.rs[:, g:g + 1],
                              ALU.subtract, ALU.mult).then_inc(done, 1)


class Ffn:

    DVE_STEPS = 2 * G

    def __init__(self, nc, ctx, tag, w, psT, psM, psO):
        def sb(name, shape):
            return ctx.enter_context(nc.sbuf_tensor(f"{tag}_{name}", shape, F32))

        def sem(name):
            return ctx.enter_context(nc.semaphore(f"{tag}_{name}"))

        self.w, self.psT, self.psM, self.psO = w, psT, psM, psO
        self.xn = sb("xn", [P, G, D])
        self.xb = sb("xb", [P, G, D])
        self.xT = sb("xT", [P, KD, COLS])
        self.g = sb("g", [P, KH, COLS])
        self.norm = RowNorm(nc, ctx, f"{tag}_ln", 1e-5, w.mhalf[:], w.consts)
        self.chain = sem("dve_chain")
        self.kept = sem("kept")
        self.xn_ready = sem("xn_ready")
        self.xb_ready = sem("xb_ready")
        self.turned = sem("turned")
        self.xT_ready = sem("xT_ready")
        self.up_done = sem("up_done")
        self.gelu_done = sem("gelu_done")
        self.down_done = sem("down_done")
        self.scaled = sem("scaled")
        self.dst_ready = sem("dst_ready")

    def primed(self):
        return [self.turned, self.down_done, self.scaled, self.chain, self.xn_ready, self.kept,
                self.dst_ready]

    def dve_in(self, dve, src, i):
        ch = Chain(dve, self.chain, self.DVE_STEPS, i)
        self.norm.stats(dve, ch, src, i)
        dve.wait_ge(self.turned, FIRST + i * KD)
        self.norm.apply(dve, src, self.xn, i, self.xn_ready)

    def dve_keep(self, dve, src, i):
        dve.tensor_tensor(self.xb[:], src[:], self.w.b2[:].unsqueeze(1).broadcast_to([P, G, D]),
                          ALU.add).then_inc(self.kept, 1)

    def pe_in(self, pe, i):
        pe.wait_ge(self.xn_ready, FIRST + i * G + G)
        for k in range(KD):
            for g in range(G):
                mm = pe.transpose(self.psT[:, k, g * P:(g + 1) * P], self.xn[:, g, k * P:(k + 1) * P],
                                  self.w.ident[:])
            mm.then_inc(self.turned, 1)

    def act_in(self, act, i):
        for k in range(KD):
            act.wait_ge(self.turned, FIRST + i * KD + k + 1)
            act.activation(self.xT[:, k, :], self.psT[:, k, :], ACT.Copy).then_inc(self.xT_ready, 1)

    def pe_up(self, pe, i):
        pe.wait_ge(self.xT_ready, i * KD + KD)
        for m in range(KH):
            if m >= 2:
                pe.wait_ge(self.gelu_done, i * KH + m - 1)
            for k in range(KD):
                mm = pe.matmul(self.psM[:, m % 2, :], self.w.s1[:, k, m * P:(m + 1) * P], self.xT[:, k, :],
                               start=(k == 0), stop=(k == KD - 1))
            mm.then_inc(self.up_done, 1)

    def act_up(self, act, i):
        for m in range(KH):
            act.wait_ge(self.up_done, i * KH + m + 1)
            if m == 0:
                act.wait_ge(self.down_done, FIRST + i)
            act.activation(self.g[:, m, :], self.psM[:, m % 2, :], ACT.Gelu, bias=self.w.b1[:, m:m + 1],
                           scale=self.w.a1[:, m:m + 1]).then_inc(self.gelu_done, 1)

    def pe_down(self, pe, i):
        pe.wait_ge(self.gelu_done, i * KH + KH)
        pe.wait_ge(self.scaled, FIRST + i)
        for g in range(G):
            for k in range(KH):
                mm = pe.matmul(self.psO[:, g, :], self.g[:, k, g * P:(g + 1) * P], self.w.s2[:, k, :],
                               start=(k == 0), stop=(k == KH - 1))
        mm.then_inc(self.down_done, 1)

    def dve_out(self, dve, dst, i):
        dve.wait_ge(self.down_done, FIRST + i + 1)
        dve.tensor_tensor(dst[:], self.psO[:], self.w.a2[:].unsqueeze(1).broadcast_to([P, G, D]),
                          ALU.mult).then_inc(self.scaled, 1)
        dve.wait_ge(self.scaled, FIRST + i + 1)
        dve.wait_ge(self.kept, FIRST + i + 1)
        dve.tensor_tensor(dst[:], dst[:], self.xb[:], ALU.add).then_inc(self.dst_ready, 1)


def pre_stage(nc, dram):
    with ExitStack() as ctx:
        def sb(name, shape):
            return ctx.enter_context(nc.sbuf_tensor(name, shape, F32))

        def sem(name):
            return ctx.enter_context(nc.semaphore(name))

        psT = ctx.enter_context(nc.psum_tensor("p_psT", [P, KD, COLS], F32))
        psM = ctx.enter_context(nc.psum_tensor("p_psM", [P, 2, COLS], F32))
        psB = ctx.enter_context(nc.psum_tensor("p_psB", [P, 2, COLS], F32))
        psO = ctx.enter_context(nc.psum_tensor("p_psO", [P, G, D], F32))
        w = FfnWeights(nc, ctx, dram, "fa")
        ffn = Ffn(nc, ctx, "fa", w, psT, psM, psO)
        ln2 = RowNorm(nc, ctx, "ln2", 1e-5, w.mhalf[:], w.consts)

        win = sb("win", [P, KD, 2 * E])
        wdt = sb("wdt", [P, KE, E])
        wbc = sb("wbc", [P, KE, 2 * N])
        convw = sb("convw", [P, KE, TAPS])
        convb = sb("convb", [P, KE])
        bdt = sb("bdt", [P, KE])
        normw = sb("normw", [P, KD])
        dtbias = sb("dtbias", [P, 1])
        xt = sb("xt", [P, G, D])
        x1 = sb("x1", [P, G, D])
        z = sb("z", [P, G, D])
        r = sb("r", [P, G, D])
        zn = sb("zn", [P, G, D])
        sq = sb("sq", [P, G, D])
        ss = sb("ss", [P, G])
        v2 = sb("v2", [P, G])
        rr = sb("rr", [P, G])
        zT = sb("zT", [P, KD, COLS])
        xbuf = sb("xbuf", [P, KE, B, TAPS - 1 + TT])
        sg = sb("sg", [P, KE, COLS])
        cv = sb("cv", [P, KE, COLS])
        xc = sb("xc", [P, KE, COLS])
        v = sb("v", [P, KE, COLS])
        e = sb("e", [P, KE, COLS])
        dt = sb("dt", [P, KE, COLS])
        u = sb("u", [P, KE, COLS])
        bcs = sb("bcs", [2 * N, COLS])
        w1n = u[:].rearrange("p a (c k) -> p (a c) k", k=D)
        w2abs = v[:].rearrange("p a (c k) -> p (a c) k", k=D)
        pad = cv

        p_loaded = sem("p_loaded")
        bias_set = sem("bias_set")
        padded = sem("padded")
        pad_zero = sem("pad_zero")
        x_in = sem("x_in")
        z_ready = sem("z_ready")
        r_ready = sem("r_ready")
        ms_ready = sem("ms_ready")
        rms_ready = sem("rms_ready")
        zn_ready = sem("zn_ready")
        z_turned = sem("z_turned")
        zT_ready = sem("zT_ready")
        proj_done = sem("proj_done")
        proj_read = sem("proj_read")
        conv_done = sem("conv_done")
        halo_done = sem("halo_done")
        xc_ready = sem("xc_ready")
        act_chain = sem("act_chain")
        dve_chain = sem("p_dve_chain")
        sp_ready = sem("sp_ready")
        th_ready = sem("th_ready")
        l_ready = sem("l_ready")
        dt_ready = sem("dt_ready")
        u_ready = sem("u_ready")
        r_out, sg_out, xc_out, bc_out, dt_out, u_out = (
            sem(n) for n in ("r_out", "sg_out", "xc_out", "bc_out", "dt_out", "u_out"))

        prime(nc, ffn.primed() + [zT_ready, proj_read, sg_out, xc_out, r_ready, u_ready, dt_ready, bc_out, r_out, z_turned,
                                  xc_ready, dt_out, u_out, act_chain, dve_chain])
        DVE_B = 2 * G + G + (TAPS - 1) * KE + 1
        ACT_B = 2
        NP = 2 * KE + KE + 1

        def steps(i):
            return bass.ds(i * TT, TT)

        with nc.Block() as block:
            @block.sync
            def _(sp):
                w.load(sp, w1n)
                for dst, src in ((win[:], dram["winT"].rearrange("(k p) m -> p k m", p=P)),
                                 (wdt[:], dram["wdtT"].rearrange("(k p) m -> p k m", p=P)),
                                 (wbc[:], dram["wbcT"].rearrange("(k p) m -> p k m", p=P)),
                                 (convw[:], dram["convw"]), (convb[:], dram["convb"]),
                                 (bdt[:], dram["bdt"]), (normw[:], dram["normw"])):
                    sp.dma_start(dst, src).then_inc(p_loaded, 16)
                sp.wait_ge(pad_zero, 1)
                n = LP - L
                zero = pad[:].rearrange("p a c -> p (a c)")[:, 0:KE * B * n].rearrange("p (a c) -> p a c", c=n)
                sp.dma_start(dram["dt"][:, :, L:LP], zero).then_inc(padded, 16)
                sp.dma_start(dram["u"][:, :, L:LP], zero).then_inc(padded, 16)
                sp.dma_start(dram["bc"][:, :, L:LP], zero[0:2 * N, 0:B, :]).then_inc(padded, 16)
                def load_x(i):
                    hold(sp, (w.loaded, 80), ffn.xn_ready, FIRST + i * G)
                    hold(sp, (w.loaded, 80), ffn.kept, FIRST + i)
                    for b in range(B):
                        sp.dma_start(xt[:, 2 * b:2 * b + 2, :],
                                     dram["x"][b, steps(i), :].rearrange("(h p) d -> p h d", p=P)
                                     ).then_inc(x_in, 16)

                def store(name, tile, done, i):
                    sp.dma_start(dram[name][:, :, steps(i)],
                                 tile.rearrange("p a (b t) -> p (a b) t", b=B)).then_inc(done, 16)

                def body(i, ahead):
                    if ahead == 2:
                        load_x(i + 2)
                    hold(sp, (w.loaded, 80), r_ready, FIRST + i + 1)
                    for b in range(B):
                        sp.dma_start(dram["r"][b, steps(i), :].rearrange("(h p) d -> p h d", p=P),
                                     r[:, 2 * b:2 * b + 2, :]).then_inc(r_out, 16)
                    hold(sp, (w.loaded, 80), proj_read, FIRST + i * NP + 2 * KE)
                    store("sg", sg[:], sg_out, i)
                    hold(sp, (w.loaded, 80), xc_ready, FIRST + i + 1)
                    store("xc", xc[:], xc_out, i)
                    hold(sp, (w.loaded, 80), proj_read, FIRST + i * NP + NP)
                    sp.dma_start(dram["bc"][:, :, steps(i)],
                                 bcs[:].rearrange("p (b t) -> p b t", b=B)).then_inc(bc_out, 16)
                    hold(sp, (w.loaded, 80), dt_ready, FIRST + i + 1)
                    store("dt", dt[:], dt_out, i)
                    hold(sp, (w.loaded, 80), u_ready, FIRST + i + 1)
                    store("u", u[:], u_out, i)

                load_x(0)
                load_x(1)
                with sp.Fori(0, TILES - 2) as i:
                    body(i, 2)
                body(TILES - 2, 1)
                body(TILES - 1, 0)
                sp.wait_ge(padded, 48)
                for s, n in ((r_out, 32), (sg_out, 16), (xc_out, 16), (bc_out, 16), (dt_out, 16), (u_out, 16)):
                    sp.wait_ge(s, FIRST + n * TILES)

            @block.gpsimd
            def _(pool):
                w.on_pool(pool)

                def body(i, ahead):
                    ln2.on_pool(pool, i)
                    pool.wait_ge(ms_ready, i + 1)
                    pool.tensor_tensor(rr[:], v2[:], w.mhalf[:], ALU.pow).then_inc(rms_ready, 1)
                    if ahead == 2:
                        ffn.norm.on_pool(pool, i + 2)

                ffn.norm.on_pool(pool, 0)
                ffn.norm.on_pool(pool, 1)
                with pool.Fori(0, TILES - 2) as i:
                    body(i, 2)
                body(TILES - 2, 1)
                body(TILES - 1, 0)

            @block.tensor
            def _(pe):
                w.on_pe(pe, w2abs, psO[:, 0, :])
                pe.wait_ge(w.signs, 2)
                pe.wait_ge(w.ready, 3)
                pe.wait_ge(p_loaded, 16 * 7)
                def body(i, ahead):
                    if ahead:
                        pe.wait_ge(zT_ready, FIRST + i * KD)
                        ffn.pe_in(pe, i + 1)
                        ffn.pe_up(pe, i + 1)
                    pe.wait_ge(zn_ready, i * G + G)
                    for k in range(KD):
                        for g in range(G):
                            mm = pe.transpose(psT[:, k, g * P:(g + 1) * P], zn[:, g, k * P:(k + 1) * P],
                                              w.ident[:])
                        mm.then_inc(z_turned, 1)
                    pe.wait_ge(zT_ready, FIRST + i * KD + KD)
                    for m in range(2 * KE):
                        pe.wait_ge(proj_read, FIRST + (i * NP + m - 1 if m >= 2 else i * NP))
                        for k in range(KD):
                            mm = pe.matmul(psB[:, m % 2, :], win[:, k, m * P:(m + 1) * P], zT[:, k, :],
                                           start=(k == 0), stop=(k == KD - 1))
                        mm.then_inc(proj_done, 1)
                    if ahead:
                        ffn.pe_down(pe, i + 1)
                    pe.wait_ge(xc_ready, FIRST + i + 1)
                    for m in range(KE):
                        pe.wait_ge(proj_read, FIRST + i * NP + 2 * KE + m - 1)
                        for k in range(KE):
                            mm = pe.matmul(psB[:, m % 2, :], wdt[:, k, m * P:(m + 1) * P], xc[:, k, :],
                                           start=(k == 0), stop=(k == KE - 1))
                        mm.then_inc(proj_done, 1)
                    pe.wait_ge(proj_read, FIRST + i * NP + 3 * KE - 1)
                    for k in range(KE):
                        mm = pe.matmul(psB[0:2 * N, 0, :], wbc[:, k, :], xc[:, k, :],
                                       start=(k == 0), stop=(k == KE - 1))
                    mm.then_inc(proj_done, 1)

                ffn.pe_in(pe, 0)
                ffn.pe_up(pe, 0)
                ffn.pe_down(pe, 0)
                with pe.Fori(0, TILES - 2) as i:
                    body(i, 2)
                body(TILES - 2, 1)
                body(TILES - 1, 0)

            @block.scalar
            def _(act):
                w.on_act(act, w1n, w2abs)
                act.wait_ge(w.ready, 3)
                act.wait_ge(p_loaded, 16 * 7)
                act.wait_ge(bias_set, 1)
                def body(i, ahead):
                    ch = Chain(act, act_chain, ACT_B, i)
                    if ahead:
                        ffn.act_in(act, i + 1)
                        ffn.act_up(act, i + 1)
                    for k in range(KD):
                        act.wait_ge(z_turned, FIRST + i * KD + k + 1)
                        act.activation(zT[:, k, :], psT[:, k, :], ACT.Copy,
                                       scale=normw[:, k:k + 1]).then_inc(zT_ready, 1)
                    act.wait_ge(halo_done, i + 1)
                    act.wait_ge(sg_out, FIRST + i * 16)
                    for m in range(2 * KE):
                        act.wait_ge(proj_done, i * NP + m + 1)
                        if m < KE:
                            act.activation(xbuf[:, m, :, TAPS - 1:], psB[:, m % 2, :].rearrange("p (b t) -> p b t", b=B),
                                           ACT.Copy).then_inc(proj_read, 1)
                        else:
                            act.activation(sg[:, m - KE, :], psB[:, m % 2, :], ACT.Silu).then_inc(proj_read, 1)
                    act.wait_ge(conv_done, i * KE + KE)
                    act.wait_ge(xc_out, FIRST + i * 16)
                    act.wait_ge(u_ready, FIRST + i)
                    act.activation(xc[:], cv[:], ACT.Silu).then_inc(xc_ready, 1)
                    for m in range(KE):
                        act.wait_ge(proj_done, i * NP + 2 * KE + m + 1)
                        act.activation(v[:, m, :], psB[:, m % 2, :], ACT.Identity,
                                       bias=bdt[:, m:m + 1]).then_inc(proj_read, 1)
                    act.wait_ge(proj_done, i * NP + NP)
                    act.wait_ge(bc_out, FIRST + i * 16)
                    act.activation(bcs[:], psB[0:2 * N, 0, :], ACT.Copy).then_inc(proj_read, 1)
                    act.wait_ge(proj_read, FIRST + i * NP + NP - 1)
                    act.wait_ge(dt_ready, FIRST + i)
                    ch.add(act.activation(e[:], v[:], ACT.Abs))
                    ch.sync()
                    ch.add(act.activation(e[:], e[:], ACT.Exp, scale=-1.0))
                    ch.sync()
                    act.activation(e[:], e[:], ACT.Ln, bias=w.ones[:, 0:1]).then_inc(l_ready, 1)
                    act.wait_ge(sp_ready, i + 1)
                    act.activation(e[:], v[:], ACT.Tanh, scale=SHARP / (DT_HALF + 1e-8),
                                   bias=dtbias[:]).then_inc(th_ready, 1)
                    ch.done()

                ffn.act_in(act, 0)
                ffn.act_up(act, 0)
                with act.Fori(0, TILES - 2) as i:
                    body(i, 2)
                body(TILES - 2, 1)
                body(TILES - 1, 0)

            @block.vector
            def _(dve):
                dve.memset(pad[:], 0.0).then_inc(pad_zero, 1)
                dve.memset(xbuf[:, :, :, 0:TAPS - 1], 0.0).then_inc(halo_done, 1)
                dve.memset(dtbias[:], -DT_MID * SHARP / (DT_HALF + 1e-8)).then_inc(bias_set, 1)
                w.on_dve(dve, psO[:, 0, :])
                dve.wait_ge(p_loaded, 16 * 7)
                dve.wait_ge(padded, 48)
                def feed(i):
                    dve.wait_ge(x_in, i * 32 + 32)
                    ffn.dve_in(dve, xt, i)

                def body(i, ahead):
                    ch = Chain(dve, dve_chain, DVE_B, i)
                    dve.wait_ge(ffn.dst_ready, FIRST + i + 1)
                    ln2.stats(dve, ch, x1, i)
                    ln2.apply(dve, x1, z, i, z_ready)
                    dve.wait_ge(z_ready, i * G + G)
                    for g in range(G):
                        ch.add(dve.tensor_tensor_reduce(out=sq[:, g, :], in0=z[:, g, :], in1=z[:, g, :], scale=1.0,
                                                        scalar=0.0, op0=ALU.mult, op1=ALU.add,
                                                        accum_out=ss[:, g:g + 1]))
                    ch.sync()
                    dve.tensor_scalar(v2[:], ss[:], 1.0 / D, 1e-6, ALU.mult, ALU.add).then_inc(ms_ready, 1)
                    dve.wait_ge(r_out, FIRST + i * 32)
                    dve.tensor_tensor(r[:], x1[:], z[:], ALU.add).then_inc(r_ready, 1)
                    dve.wait_ge(rms_ready, i + 1)
                    dve.wait_ge(z_turned, FIRST + i * KD)
                    for g in range(G):
                        dve.tensor_scalar(zn[:, g, :], z[:, g, :], rr[:, g:g + 1], None,
                                          ALU.mult).then_inc(zn_ready, 1)
                    dve.wait_ge(proj_read, FIRST + i * NP + KE)
                    dve.wait_ge(xc_ready, FIRST + i)
                    for tap in range(TAPS):
                        for c in range(KE):
                            out = cv[:, c, :].rearrange("p (b t) -> p b t", b=B)
                            src = xbuf[:, c, :, tap:tap + TT]
                            if tap == 0:
                                ins = dve.tensor_scalar(out, src, convw[:, c, 0:1], convb[:, c:c + 1],
                                                        ALU.mult, ALU.add)
                            else:
                                ins = dve.scalar_tensor_tensor(out=out, in0=src, scalar=convw[:, c, tap:tap + 1],
                                                               in1=out, op0=ALU.mult, op1=ALU.add)
                            if tap == TAPS - 1:
                                ins.then_inc(conv_done, 1)
                            else:
                                ch.add(ins)
                        if tap < TAPS - 1:
                            ch.sync()
                    dve.wait_ge(conv_done, i * KE + KE)
                    ch.add(dve.tensor_copy(sq[:, 0, 0:KE * B * (TAPS - 1)].rearrange("p (c b t) -> p c b t", c=KE, b=B),
                                           xbuf[:, :, :, TT:]))
                    ch.sync()
                    dve.tensor_copy(xbuf[:, :, :, 0:TAPS - 1],
                                    sq[:, 0, 0:KE * B * (TAPS - 1)].rearrange("p (c b t) -> p c b t", c=KE, b=B)
                                    ).then_inc(halo_done, 1)
                    dve.wait_ge(halo_done, i + 2)
                    if ahead:
                        if ahead == 2:
                            feed(i + 2)
                        dve.wait_ge(r_ready, FIRST + i + 1)
                        ffn.dve_out(dve, x1, i + 1)
                        if ahead == 2:
                            dve.wait_ge(ffn.dst_ready, FIRST + i + 2)
                            ffn.dve_keep(dve, xt, i + 2)
                    dve.wait_ge(l_ready, i + 1)
                    dve.scalar_tensor_tensor(out=v[:], in0=v[:], scalar=0.0, in1=e[:], op0=ALU.max,
                                             op1=ALU.add).then_inc(sp_ready, 1)
                    dve.wait_ge(th_ready, i + 1)
                    dve.wait_ge(dt_out, FIRST + i * 16)
                    dve.tensor_scalar(dt[:], e[:], DT_HALF / SHARP, DT_MID, ALU.mult, ALU.add).then_inc(dt_ready, 1)
                    dve.wait_ge(dt_ready, FIRST + i + 1)
                    dve.wait_ge(u_out, FIRST + i * 16)
                    dve.tensor_tensor(u[:], dt[:], xc[:], ALU.mult).then_inc(u_ready, 1)
                    ch.done()

                feed(0)
                ffn.dve_keep(dve, xt, 0)
                feed(1)
                ffn.dve_out(dve, x1, 0)
                dve.wait_ge(ffn.dst_ready, FIRST + 1)
                ffn.dve_keep(dve, xt, 1)
                with dve.Fori(0, TILES - 2) as i:
                    body(i, 2)
                body(TILES - 2, 1)
                body(TILES - 1, 0)


def scan_stage(nc, dram):
    with ExitStack() as ctx:
        def sb(name, shape):
            return ctx.enter_context(nc.sbuf_tensor(name, shape, F32))

        def sem(name):
            return ctx.enter_context(nc.semaphore(name))

        decay = sb("decay", [P, 2, CB, ROWS * W])
        dtc = sb("dtc", [P, KE * B, CT])
        uc = [sb(f"uc{h}", [P, KE * B, HALF]) for h in range(2)]
        bc = [sb(f"bc{q}", [P, 2, B * N, S]) for q in range(3)]
        inp = sb("inp", [P, ROWS, W])
        h = sb("h", [P, ROWS, W])
        hc = sb("hc", [P, 2, ROWS, 2 * S])
        yc = sb("yc", [P, KE * B, CT])
        a16 = sb("a16", [P, KE * N])
        ones = sb("sc_ones", [P, P])
        ident = sb("sc_ident", [P, P])
        sq = sb("sc_sq", [P, B, KE * N])
        ss = sb("sc_ss", [P, B])
        qs = sb("qs", [P, B])
        nrm = sb("nrm", [P, B])
        cl = sb("cl", [P, B])
        rc = sb("rc", [P, B])
        phalf = sb("phalf", [P, B])
        u0 = sb("u0", [P, KE * B, 2])
        b0 = sb("b0", [P, B, N, 2])
        psQ = ctx.enter_context(nc.psum_tensor("psQ", [P, 512], F32))
        psY = ctx.enter_context(nc.psum_tensor("psY", [P, 2, 512], F32))

        s_in = sem("s_in")
        dt_in = sem("dt_in")
        u_in = [sem(f"u_in{q}") for q in range(2)]
        bc_in = [sem(f"bc_in{q}") for q in range(3)]
        blk_out = sem("blk_out")
        consts = sem("s_consts")
        filled = sem("s_filled")
        zeroed = sem("s_zeroed")
        a_steps = sem("a_steps")
        tanh_done = sem("tanh_done")
        decay_ready = sem("decay_ready")
        inp_ready = sem("inp_ready")
        carry_ready = sem("carry_ready")
        h_ready = sem("h_ready")
        sq_ready = sem("sq_ready")
        sum_ready = sem("sum_ready")
        sum_copied = sem("sum_copied")
        root_ready = sem("root_ready")
        norm_ready = sem("norm_ready")
        inv_ready = sem("inv_ready")
        hc_ready = sem("hc_ready")
        y_summed = sem("y_summed")
        y_copied = sem("y_copied")
        y_out = sem("y_out")

        prime(nc, [inp_ready, hc_ready, inv_ready, sum_copied, y_copied, y_out, y_summed])

        def rows(ap):
            return ap.rearrange("p (c b n) e -> p c b n e", c=KE, b=B)

        drow = decay[:].rearrange("p q k (c b n e) -> p q k c b n e", c=KE, b=B, e=W)

        NCH = KE * N
        cut = [round(q * NCH / CB) for q in range(CB + 1)]

        with nc.Block() as block:
            @block.sync
            def _(sp):
                sp.dma_start(a16[:], dram["alog"]).then_inc(s_in, 16)
                sp.dma_start(u0[:], dram["u"][:, :, 0:2]).then_inc(s_in, 16)
                for b in range(B):
                    sp.dma_start(b0[:, b], dram["bc"][0:N, b:b + 1, 0:2].rearrange("n b t -> b n t")
                                 .broadcast_to([P, N, 2])).then_inc(s_in, 16)

                def relayout(c):
                    for q in range(2):
                        for b in range(B):
                            sp.dma_start(
                                dram["blk"][bass.ds(c * CB, CB), q, b, :, :].rearrange("k n t -> n k t"),
                                dram["bc"][q * N:(q + 1) * N, b, bass.ds(c * CT + 1 - q, CT)]
                                .rearrange("n (k t) -> n k t", t=S)).then_inc(blk_out, 16)

                def load_dt(c):
                    sp.dma_start(dtc[:], dram["dt"][:, :, bass.ds(c * CT + 1, CT)]).then_inc(dt_in, 16)

                def load_u(c, half):
                    sp.dma_start(uc[half][:], dram["u"][:, :, bass.ds(c * CT + 1 + half * HALF, HALF)]
                                 ).then_inc(u_in[half], 16)

                def load_bc(j, q):
                    sp.dma_start(bc[q][:], dram["blk"][bass.ds(j, 1)].rearrange("o q b n t -> o (q b n t)")
                                 .broadcast_to([P, 2 * B * N * S])).then_inc(bc_in[q], 16)

                load_dt(0)
                relayout(0)
                load_u(0, 0)
                sp.wait_ge(blk_out, 64)
                load_bc(0, 0)
                load_bc(1, 1)

                def turn(t, slots):
                    j0 = t * BODY
                    for s in range(slots):
                        c, cs = t * 2 + s // CB, s % CB
                        more = slots == BODY or s // CB == 0
                        if cs == 0:
                            hold(sp, (s_in, 64), inp_ready, FIRST + c * CB)
                            load_u(c, 1)
                            if more:
                                hold(sp, (s_in, 64), tanh_done, c * NCH + NCH)
                                load_dt(c + 1)
                                relayout(c + 1)
                        if cs == 6 and more:
                            hold(sp, (s_in, 64), inp_ready, FIRST + c * CB + 6)
                            load_u(c + 1, 0)
                        if s + 2 < slots or slots == BODY:
                            if cs == CB - 2:
                                hold(sp, (s_in, 64), blk_out, c * 64 + 128)
                            hold(sp, (s_in, 64), hc_ready, FIRST + j0 + s)
                            load_bc(j0 + s + 2, (s + 2) % 3)
                        if s == 14:
                            hold(sp, (s_in, 64), y_copied, FIRST + t * 12 + 6)
                            sp.dma_start(dram["y"][:, :, bass.ds(t * 2 * CT, CT)], yc[:]).then_inc(y_out, 16)
                        if s == BODY - 1:
                            hold(sp, (s_in, 64), y_copied, FIRST + t * 12 + 12)
                            sp.dma_start(dram["y"][:, :, bass.ds(t * 2 * CT + CT, CT)], yc[:]).then_inc(y_out, 16)
                with sp.Fori(0, TURNS) as t:
                    turn(t, BODY)
                turn(TURNS, TAIL)
                pairs = TAIL // 2
                sp.wait_ge(y_copied, FIRST + TURNS * 12 + 6)
                sp.dma_start(dram["y"][:, :, TURNS * 2 * CT:TURNS * 2 * CT + CT], yc[:]).then_inc(y_out, 16)
                sp.wait_ge(y_copied, FIRST + TURNS * 12 + pairs)
                last = TAIL * S - CT
                sp.dma_start(dram["y"][:, :, TURNS * 2 * CT + CT:TURNS * 2 * CT + CT + last],
                             yc[:, :, 0:last]).then_inc(y_out, 16)
                sp.wait_ge(y_out, FIRST + 16 * (2 * TURNS + 2))

            @block.gpsimd
            def _(pool):
                pool.memset(ident[:], 0.0).then_inc(filled, 1)
                pool.memset(ones[:], 1.0).then_inc(filled, 1)
                pool.memset(phalf[:], 0.5).then_inc(filled, 1)
                pool.wait_ge(filled, 3)
                pool.affine_select(out=ident[:], in_=ident[:], compare_op=ALU.not_equal, fill=1.0,
                                   base=0, pattern=[[-1, P]], channel_multiplier=1).then_inc(consts, 1)
                with pool.Fori(0, TURNS * BODY + TAIL) as c:
                    pool.wait_ge(sum_copied, FIRST + c + 1)
                    pool.tensor_tensor(nrm[:], qs[:], phalf[:], ALU.pow).then_inc(root_ready, 1)
                    hold(pool, (filled, 3), root_ready, c + 1)
                    pool.wait_ge(inv_ready, FIRST + c)
                    pool.tensor_scalar(cl[:], nrm[:], 1e-8, 20.0, ALU.add, ALU.max).then_inc(norm_ready, 1)

            @block.tensor
            def _(pe):
                pe.wait_ge(consts, 1)

                def total(c):
                    pe.wait_ge(sq_ready, c * B + B)
                    pe.wait_ge(sum_copied, FIRST + c)
                    pe.matmul(psQ[:, 0:B], ones[:], ss[:], start=True, stop=True).then_inc(sum_ready, 1)

                def readout(p, pl, n0, n1):
                    if n0 == 0:
                        pe.wait_ge(hc_ready, FIRST + p * 2 + 2)
                        pe.wait_ge(y_copied, FIRST + (p - 1 if pl >= 2 else (p if pl == 0 else p - 1)))
                    for n in range(n0, n1):
                        rhs = hc[:, pl % 2].rearrange("p (c n) t -> p c n t", n=N)[:, :, n, :]
                        mm = pe.matmul(psY[:, pl % 2, 0:KE * B * 2 * S], ident[:], rhs,
                                       start=(n == 0), stop=(n == N - 1))
                    if n1 == N:
                        mm.then_inc(y_summed, 1)

                total(0)

                def turn(t, slots):
                    for s in range(slots):
                        if not (slots == TAIL and s == slots - 1):
                            total(t * BODY + s + 1)
                        if s % 2 == 0 and s > 0:
                            readout(t * 12 + s // 2 - 1, s // 2 - 1, N // 2, N)
                        if s % 2 == 1:
                            last = s == slots - 1
                            readout(t * 12 + s // 2, s // 2, 0, N if last else N // 2)
                with pe.Fori(0, TURNS) as t:
                    turn(t, BODY)
                turn(TURNS, TAIL)

            @block.scalar
            def _(act):
                act.wait_ge(s_in, 64)
                act.activation(a16[:], a16[:], ACT.Tanh, scale=SHARP / (A_HALF + 1e-8)).then_inc(a_steps, 1)
                act.wait_ge(a_steps, 1)
                act.activation(a16[:], a16[:], ACT.Exp, scale=A_HALF / SHARP).then_inc(a_steps, 1)
                act.wait_ge(a_steps, 3)

                def tanhs(c, q, lo, hi, blocks=CB):
                    for m in range(lo, hi):
                        k, n = m // N, m % N
                        act.activation(drow[:, q, 0:blocks, k, :, n, 1:].rearrange("p k b e -> p b k e"),
                                       dtc[:, k * B:(k + 1) * B, 0:blocks * S].rearrange("p b (k e) -> p b k e", e=S),
                                       ACT.Tanh, scale=a16[:, m:m + 1]).then_inc(tanh_done, 1)

                def decays(q, k):
                    ap = decay[:, q, k, :].rearrange("p (r e) -> p r e", e=W)[:, :, 1:]
                    act.activation(ap, ap, ACT.Exp, scale=DTA_HALF / SHARP).then_inc(decay_ready, 1)

                def copy_y(t, pl):
                    if pl % 6 == 0:
                        act.wait_ge(y_out, FIRST + t * 32 + pl // 6 * 16)
                    act.wait_ge(y_summed, FIRST + t * PAIRS_BODY + pl + 1)
                    act.activation(yc[:, :, (pl % 6) * 2 * S:(pl % 6 + 1) * 2 * S],
                                   psY[:, pl % 2, 0:KE * B * 2 * S].rearrange("p (c t) -> p c t", t=2 * S),
                                   ACT.Copy).then_inc(y_copied, 1)

                act.wait_ge(dt_in, 16)
                tanhs(0, 0, 0, NCH)
                act.wait_ge(tanh_done, NCH)
                decays(0, 0)

                def turn(t, slots):
                    for s in range(slots):
                        c, cs, q = t * 2 + s // CB, s % CB, s // CB
                        more = slots == BODY or s // CB == 0
                        if cs == 0 and more:
                            act.wait_ge(dt_in, c * 16 + 32)
                            act.wait_ge(h_ready, c * CB + 1)
                        if cs < CB - 1 and s + 1 < slots:
                            decays(q, cs + 1)
                        if more:
                            tanhs(c + 1, 1 - q, cut[cs], cut[cs + 1],
                                  CB if slots == BODY else TAIL - CB)
                        if cs == CB - 1:
                            act.wait_ge(tanh_done, c * NCH + 2 * NCH)
                            decays(1 - q, 0)
                        if s % 2 == 1 and s >= 3:
                            copy_y(t, s // 2 - 1)
                        if s == slots - 1:
                            copy_y(t, s // 2)
                with act.Fori(0, TURNS) as t:
                    turn(t, BODY)
                turn(TURNS, TAIL)

            @block.vector
            def _(dve):
                dve.memset(decay[:, 0].rearrange("p k (r e) -> p k r e", e=W)[:, :, :, 0], 0.0).then_inc(zeroed, 1)
                dve.memset(decay[:, 1].rearrange("p k (r e) -> p k r e", e=W)[:, :, :, 0], 0.0).then_inc(zeroed, 1)
                dve.wait_ge(a_steps, 2)
                dve.tensor_scalar(a16[:], a16[:], -SHARP / (DTA_HALF + 1e-8), None, ALU.mult).then_inc(a_steps, 1)
                dve.wait_ge(zeroed, 2)
                dve.wait_ge(filled, 3)

                dve.wait_ge(s_in, 64)
                dve.tensor_tensor(
                    h[:, :, S].rearrange("p (c b n) -> p c b n", c=KE, b=B),
                    u0[:, :, 0].rearrange("p (c b) -> p c b", b=B).unsqueeze(3).broadcast_to([P, KE, B, N]),
                    b0[:, :, :, 0].unsqueeze(1).broadcast_to([P, KE, B, N]),
                    ALU.mult).then_inc(h_ready, 1)

                def squares(c):
                    dve.wait_ge(h_ready, c + 1)
                    for b in range(B):
                        last = rows(h[:])[:, :, b, :, S]
                        dve.tensor_tensor_reduce(out=sq[:, b, :].rearrange("p (c n) -> p c n", c=KE), in0=last, in1=last,
                                                 scale=1.0, scalar=0.0, op0=ALU.mult, op1=ALU.add,
                                                 accum_out=ss[:, b:b + 1]).then_inc(sq_ready, 1)

                def copy_sum(c):
                    dve.wait_ge(sum_ready, c + 1)
                    dve.tensor_copy(qs[:], psQ[:, 0:B]).then_inc(sum_copied, 1)

                def inputs(k, q):
                    half, o = k // 6, k % 6 * S
                    dve.tensor_tensor(
                        inp[:, :, 1:].rearrange("p (c n) e -> p c n e", c=KE * B),
                        uc[half][:, :, o:o + S].unsqueeze(2).broadcast_to([P, KE * B, N, S]),
                        bc[q][:, 0].unsqueeze(1).broadcast_to([P, KE, B * N, S]),
                        ALU.mult).then_inc(inp_ready, 1)

                def scan(k, q, j):
                    dve.wait_ge(norm_ready, j + 1)
                    dve.reciprocal(rc[:], cl[:]).then_inc(inv_ready, 1)
                    dve.wait_ge(inv_ready, FIRST + j + 1)
                    for b in range(B):
                        dve.tensor_scalar(rows(inp[:])[:, :, b, :, 0], rows(h[:])[:, :, b, :, S], rc[:, b:b + 1], 20.0,
                                          ALU.mult, ALU.mult).then_inc(carry_ready, 1)
                    dve.wait_ge(carry_ready, j * B + B)
                    dve.wait_ge(inp_ready, FIRST + j + 1)
                    dve.wait_ge(decay_ready, j + 1)
                    dve.wait_ge(hc_ready, FIRST + j)
                    dve.tensor_tensor_scan(h[:].rearrange("p r e -> p (r e)"),
                                           decay[:, q, k, :], inp[:].rearrange("p r e -> p (r e)"),
                                           0.0, ALU.mult, ALU.add).then_inc(h_ready, 1)

                squares(0)
                copy_sum(0)
                dve.wait_ge(u_in[0], 16)
                dve.wait_ge(bc_in[0], 16)
                inputs(0, 0)

                def turn(t, slots):
                    for s in range(slots):
                        j, c, cs, q = t * BODY + s, t * 2 + s // CB, s % CB, s // CB
                        last = slots == TAIL and s == slots - 1
                        scan(cs, q, j)
                        if not last:
                            squares(j + 1)
                        else:
                            dve.wait_ge(h_ready, j + 2)
                        pl = s // 2
                        if s % 2 == 0 and pl >= 2:
                            dve.wait_ge(y_summed, FIRST + t * 12 + pl - 1)
                        elif s % 2 == 0:
                            dve.wait_ge(y_summed, FIRST + t * 12)
                        dve.tensor_tensor(
                            hc[:, pl % 2, :, s % 2 * S:(s % 2 + 1) * S].rearrange("p (c r) e -> p c r e", c=KE),
                            h[:, :, 0:S].rearrange("p (c r) e -> p c r e", c=KE),
                            bc[s % 3][:, 1].unsqueeze(1).broadcast_to([P, KE, B * N, S]),
                            ALU.mult).then_inc(hc_ready, 1)
                        if last:
                            continue
                        copy_sum(j + 1)
                        k = (cs + 1) % CB
                        if k == 0:
                            dve.wait_ge(u_in[0], c * 16 + 32)
                        if k == 6:
                            dve.wait_ge(u_in[1], c * 16 + 16)
                        r, turns = (s + 1) % 3, t * 8 + (s + 1) // 3 + 1
                        dve.wait_ge(bc_in[r], turns * 16)
                        inputs(k, r)
                with dve.Fori(0, TURNS) as t:
                    turn(t, BODY)
                turn(TURNS, TAIL)


def post_stage(nc, dram, out):
    with ExitStack() as ctx:
        def sb(name, shape):
            return ctx.enter_context(nc.sbuf_tensor(name, shape, F32))

        def sem(name):
            return ctx.enter_context(nc.semaphore(name))

        psT = ctx.enter_context(nc.psum_tensor("q_psT", [P, KD, COLS], F32))
        psM = ctx.enter_context(nc.psum_tensor("q_psM", [P, 2, COLS], F32))
        psX = ctx.enter_context(nc.psum_tensor("q_psX", [P, G, D], F32))
        psO = ctx.enter_context(nc.psum_tensor("q_psO", [P, G, D], F32))
        w = FfnWeights(nc, ctx, dram, "fb")
        ffn = Ffn(nc, ctx, "fb", w, psT, psM, psO)
        wout = sb("wout", [P, KE, D])
        dpar = sb("dpar", [P, KE])
        rscale = sb("rscale", [P, 1])
        ys = sb("ys", [P, KE, COLS])
        xc = sb("q_xc", [P, KE, COLS])
        sg = sb("q_sg", [P, KE, COLS])
        r = sb("q_r", [P, G, D])
        x2 = sb("x2", [P, G, D])
        res = sb("res", [P, G, D])
        w1n = sb("q_w1n", [P, KH, D])
        w2abs = sb("q_w2abs", [P, KH, D])
        q_loaded = sem("q_loaded")
        scale_steps = sem("scale_steps")
        y_in, xc_in, sg_in, r_in = (sem(n) for n in ("q_y_in", "q_xc_in", "q_sg_in", "q_r_in"))
        skip_added = sem("skip_added")
        gated = sem("gated")
        out_done = sem("out_done")
        x2_ready = sem("x2_ready")
        stored = sem("stored")
        prime(nc, ffn.primed() + [skip_added, gated, out_done, x2_ready, stored])

        def steps(i):
            return bass.ds(i * TT, TT)

        with nc.Block() as block:
            @block.sync
            def _(sp):
                w.load(sp, w1n)
                sp.dma_start(wout[:], dram["woutT"].rearrange("(k p) m -> p k m", p=P)).then_inc(q_loaded, 16)
                sp.dma_start(dpar[:], dram["dpar"]).then_inc(q_loaded, 16)
                sp.dma_start(rscale[:], dram["rscale"].broadcast_to([P, 1])).then_inc(q_loaded, 16)
                def load(name, tile, done, i):
                    sp.dma_start(tile[:].rearrange("p a (b t) -> p (a b) t", b=B),
                                 dram[name][:, :, steps(i)]).then_inc(done, 16)

                def fetch(i):
                    hold(sp, (w.loaded, 80), skip_added, FIRST + i * KE)
                    load("xc", xc, xc_in, i)
                    hold(sp, (w.loaded, 80), gated, FIRST + i)
                    load("sg", sg, sg_in, i)
                    hold(sp, (w.loaded, 80), out_done, FIRST + i)
                    load("y", ys, y_in, i)
                    hold(sp, (w.loaded, 80), x2_ready, FIRST + i)
                    for b in range(B):
                        sp.dma_start(r[:, 2 * b:2 * b + 2, :],
                                     dram["r"][b, steps(i), :].rearrange("(h p) d -> p h d", p=P)).then_inc(r_in, 16)

                def store(i):
                    hold(sp, (w.loaded, 80), ffn.dst_ready, FIRST + i + 1)
                    for b in range(B):
                        sp.dma_start(out[b, steps(i), :].rearrange("(h p) d -> p h d", p=P),
                                     res[:, 2 * b:2 * b + 2, :]).then_inc(stored, 16)

                fetch(0)
                with sp.Fori(0, TILES - 1) as i:
                    fetch(i + 1)
                    store(i)
                store(TILES - 1)
                sp.wait_ge(stored, FIRST + 32 * TILES)

            @block.gpsimd
            def _(pool):
                w.on_pool(pool)
                with pool.Fori(0, TILES) as i:
                    ffn.norm.on_pool(pool, i)

            @block.tensor
            def _(pe):
                w.on_pe(pe, w2abs, psO[:, 0, :])
                pe.wait_ge(w.signs, 2)
                pe.wait_ge(w.ready, 3)
                pe.wait_ge(q_loaded, 48)

                def project(i):
                    pe.wait_ge(gated, FIRST + i + 1)
                    pe.wait_ge(x2_ready, FIRST + i)
                    for g in range(G):
                        for k in range(KE):
                            mm = pe.matmul(psX[:, g, :], ys[:, k, g * P:(g + 1) * P], wout[:, k, :],
                                           start=(k == 0), stop=(k == KE - 1))
                    mm.then_inc(out_done, 1)

                def body(i, ahead):
                    ffn.pe_in(pe, i)
                    ffn.pe_up(pe, i)
                    if ahead:
                        project(i + 1)
                    ffn.pe_down(pe, i)

                project(0)
                with pe.Fori(0, TILES - 1) as i:
                    body(i, True)
                body(TILES - 1, False)

            @block.scalar
            def _(act):
                w.on_act(act, w1n, w2abs)
                act.wait_ge(q_loaded, 48)
                act.activation(rscale[:], rscale[:], ACT.Exp, scale=-1.0).then_inc(scale_steps, 1)
                act.wait_ge(w.ready, 3)
                with act.Fori(0, TILES) as i:
                    ffn.act_in(act, i)
                    ffn.act_up(act, i)

            @block.vector
            def _(dve):
                w.on_dve(dve, psO[:, 0, :])
                dve.wait_ge(q_loaded, 48)
                dve.wait_ge(scale_steps, 1)
                dve.tensor_scalar(rscale[:], rscale[:], 1.0, None, ALU.add).then_inc(scale_steps, 1)
                dve.wait_ge(scale_steps, 2)
                dve.reciprocal(rscale[:], rscale[:]).then_inc(scale_steps, 1)
                dve.wait_ge(scale_steps, 3)
                dve.tensor_scalar(rscale[:], rscale[:], 0.5, None, ALU.mult).then_inc(scale_steps, 1)
                dve.wait_ge(scale_steps, 4)

                def gate(i):
                    dve.wait_ge(y_in, i * 16 + 16)
                    dve.wait_ge(xc_in, i * 16 + 16)
                    dve.wait_ge(sg_in, i * 16 + 16)
                    for k in range(KE):
                        dve.scalar_tensor_tensor(out=ys[:, k, :], in0=xc[:, k, :], scalar=dpar[:, k:k + 1],
                                                 in1=ys[:, k, :], op0=ALU.mult, op1=ALU.add).then_inc(skip_added, 1)
                    dve.wait_ge(skip_added, FIRST + i * KE + KE)
                    dve.tensor_tensor(ys[:], ys[:], sg[:], ALU.mult).then_inc(gated, 1)

                def residual(i):
                    dve.wait_ge(out_done, FIRST + i + 1)
                    dve.wait_ge(r_in, i * 32 + 32)
                    dve.wait_ge(ffn.kept, FIRST + i)
                    dve.scalar_tensor_tensor(out=x2[:], in0=psX[:], scalar=rscale[:], in1=r[:], op0=ALU.mult,
                                             op1=ALU.add).then_inc(x2_ready, 1)
                    dve.wait_ge(x2_ready, FIRST + i + 1)
                    ffn.dve_in(dve, x2, i)

                def body(i, ahead):
                    if ahead:
                        gate(i + 1)
                        residual(i + 1)
                    dve.wait_ge(stored, FIRST + i * 32)
                    ffn.dve_out(dve, res, i)
                    if ahead:
                        dve.wait_ge(ffn.dst_ready, FIRST + i + 1)
                        ffn.dve_keep(dve, x2, i + 1)

                gate(0)
                residual(0)
                ffn.dve_keep(dve, x2, 0)
                with dve.Fori(0, TILES - 1) as i:
                    body(i, True)
                body(TILES - 1, False)


def build(nc, dram, out):
    def scratch(name, shape):
        return nc.dram_tensor(f"scratch_{name}", shape, F32, kind="Internal").ap()

    dram = dict(dram)
    dram["dt"] = scratch("dt", (P, KE * B, LP))
    dram["u"] = scratch("u", (P, KE * B, LP))
    dram["xc"] = scratch("xc", (P, KE * B, L))
    dram["sg"] = scratch("sg", (P, KE * B, L))
    dram["y"] = scratch("y", (P, KE * B, LP))
    dram["bc"] = scratch("bc", (2 * N, B, LP))
    dram["blk"] = scratch("blk", (CHUNKS * CB, 2, B, N, S))
    dram["r"] = scratch("r", (B, L, D))
    pre_stage(nc, dram)
    scan_stage(nc, dram)
    post_stage(nc, dram, out)


def kernel(L0_attn_x, L0_attn_norm_w, L0_attn_W_in, L0_attn_conv_w, L0_attn_conv_b, L0_attn_W_dt, L0_attn_b_dt,
           L0_attn_W_B, L0_attn_W_C, L0_attn_A_log, L0_attn_D_param, L0_attn_W_out, L0_attn_residual_scale,
           L0_ffn_w1, L0_ffn_b1, L0_ffn_w2, L0_ffn_b2):
    import numpy as np
    import concourse.bacc as bacc
    from concourse.bass_utils import run_bass_kernel_spmd

    def a(x):
        return np.asarray(x)

    def cols(x, k):
        x = a(x).reshape(k, P, -1)
        return x.transpose(1, 0, 2).reshape(P, -1)

    ins = {
        "x": a(L0_attn_x), "normw": cols(L0_attn_norm_w, KD), "winT": a(L0_attn_W_in).T,
        "convw": cols(a(L0_attn_conv_w).reshape(E, TAPS), KE).reshape(P, KE, TAPS), "convb": cols(L0_attn_conv_b, KE),
        "wdtT": a(L0_attn_W_dt).T, "bdt": cols(L0_attn_b_dt, KE),
        "wbcT": np.concatenate([a(L0_attn_W_B), a(L0_attn_W_C)], 0).T,
        "alog": cols(L0_attn_A_log, KE), "dpar": cols(L0_attn_D_param, KE), "woutT": a(L0_attn_W_out).T,
        "rscale": a(L0_attn_residual_scale).reshape(1, 1),
        "w1": a(L0_ffn_w1), "w1T": a(L0_ffn_w1).T, "b1": cols(L0_ffn_b1, KH),
        "w2T": a(L0_ffn_w2).T, "b2": a(L0_ffn_b2).reshape(1, D),
    }
    nc = bacc.Bacc("TRN2", target_bir_lowering=False, num_devices=1)
    arrays, dram = {}, {}
    for name, x in ins.items():
        x = np.ascontiguousarray(x)
        arrays[f"in_{name}"] = x
        dram[name] = nc.dram_tensor(f"in_{name}", x.shape, mybir.dt.from_np(x.dtype), kind="ExternalInput").ap()
    out = nc.dram_tensor("out_y", (B, L, D), F32, kind="ExternalOutput").ap()
    build(nc, dram, out)
    got = run_bass_kernel_spmd(nc, [arrays], core_ids=[0])
    return got.results[0]["out_y"]
```

```python
from contextlib import ExitStack

import concourse.bass as bass
from concourse import mybir

F32 = mybir.dt.float32
ALU = mybir.AluOpType
ACT = mybir.ActivationFunctionType

P = 128
B, L, D = 2, 2048, 256
E = 512
N = 16
H = 1024
TAPS = 4
KD, KE, KH = D // P, E // P, H // P
TT = 256
TILES = L // TT
G = B * TT // P
COLS = B * TT

S = 10
W = S + 1
ROWS = KE * B * N
CB = 12
CT = CB * S
BLOCKS = -(-L // S)
PAIRS_BODY = 12
BODY = 2 * CB
TURNS = BLOCKS // BODY
TAIL = -(-(BLOCKS - TURNS * BODY) // 2) * 2
CHUNKS = 2 * TURNS + -(-TAIL // CB)
LP = ((CHUNKS + 1) * CB + 1) * S + 8
HALF = CT // 2
SPLIT = G // 2

DT_MID, DT_HALF = (0.1 + 0.001) / 2, (0.1 - 0.001) / 2
A_HALF = 5.0
DTA_HALF = 8.0
SHARP = 0.5
CLAMP = 20.0


BUFS = 2
FIRST = 1


def prime(nc, sems, bufs=()):
    engines = (nc.sync, nc.gpsimd, nc.vector, nc.scalar)
    for k, s in enumerate(sems):
        engines[k % 4].sem_inc(s, FIRST)
    for k, s in enumerate(bufs):
        engines[k % 4].sem_inc(s, BUFS)
    nc.all_engine_barrier()


class Chain:

    def __init__(self, eng, sem, per, turn):
        self.eng, self.sem, self.base, self.n, self.per = eng, sem, turn * per + FIRST, 0, per

    def add(self, ins):
        self.n += 1
        ins.then_inc(self.sem, 1)

    def sync(self):
        self.eng.wait_ge(self.sem, self.base + self.n)

    def done(self):
        assert self.n == self.per, (self.n, self.per)


def hold(eng, settled, sem, value):
    if not isinstance(value, int):
        value = eng.to_reg(value)
        eng.wait_ge(*settled)
    eng.wait_ge(sem, value)


class FfnWeights:

    def __init__(self, nc, ctx, dram, tag):
        def sb(name, shape):
            return ctx.enter_context(nc.sbuf_tensor(f"{tag}_{name}", shape, F32))

        def sem(name):
            return ctx.enter_context(nc.semaphore(f"{tag}_{name}"))

        self.dram = dram
        self.s1 = sb("s1", [P, KD, H])
        self.s2 = sb("s2", [P, KH, D])
        self.a1 = sb("a1", [P, KH])
        self.b1 = sb("b1", [P, KH])
        self.a2 = sb("a2", [P, D])
        self.b2 = sb("b2", [P, D])
        self.ident = sb("ident", [P, P])
        self.ones = sb("ones", [P, P])
        self.mhalf = sb("mhalf", [P, G])
        self.w1_in = sem("w1_in")
        self.w2_in = sem("w2_in")
        self.loaded = sem("w_loaded")
        self.abs1 = sem("w_abs1")
        self.abs2 = sem("w_abs2")
        self.sum2 = sem("w_sum2")
        self.signs = sem("w_signs")
        self.consts = sem("w_consts")
        self.filled = sem("w_filled")
        self.ready = sem("w_ready")

    def load(self, sp, w1n):
        d = self.dram
        sp.dma_start(self.s2[:], d["w2T"].rearrange("(k p) d -> p k d", p=P)).then_inc(self.w2_in, 16)
        sp.dma_start(w1n[:], d["w1"].rearrange("(m p) k -> p m k", p=P)).then_inc(self.w1_in, 16)
        sp.dma_start(self.s1[:], d["w1T"].rearrange("(k p) h -> p k h", p=P)).then_inc(self.loaded, 16)
        sp.dma_start(self.b1[:], d["b1"]).then_inc(self.loaded, 16)
        sp.dma_start(self.b2[:], d["b2"].broadcast_to([P, D])).then_inc(self.loaded, 16)

    def on_act(self, act, w1n, w2abs):
        act.wait_ge(self.w2_in, 16)
        act.activation(w2abs[:], self.s2[:], ACT.Abs).then_inc(self.abs2, 1)
        act.wait_ge(self.w1_in, 16)
        for m in range(KH):
            act.activation(w1n[:, m, :], w1n[:, m, :], ACT.Abs,
                           accum_out=self.a1[:, m:m + 1]).then_inc(self.abs1, 1)
        act.wait_ge(self.loaded, 48)
        act.activation(self.s1[:], self.s1[:], ACT.Sign).then_inc(self.signs, 1)
        act.wait_ge(self.abs2, 1)
        act.activation(self.s2[:], self.s2[:], ACT.Sign).then_inc(self.signs, 1)

    def on_pool(self, pool):
        pool.memset(self.ident[:], 0.0).then_inc(self.filled, 1)
        pool.memset(self.ones[:], 1.0).then_inc(self.filled, 1)
        pool.memset(self.mhalf[:], -0.5).then_inc(self.filled, 1)
        pool.wait_ge(self.filled, 3)
        pool.affine_select(out=self.ident[:], in_=self.ident[:], compare_op=ALU.not_equal, fill=1.0,
                           base=0, pattern=[[-1, P]], channel_multiplier=1).then_inc(self.consts, 1)

    def on_pe(self, pe, w2abs, psum):
        pe.wait_ge(self.consts, 1)
        pe.wait_ge(self.abs2, 1)
        for k in range(KH):
            mm = pe.matmul(psum, self.ones[:], w2abs[:, k, :], start=(k == 0), stop=(k == KH - 1))
        mm.then_inc(self.sum2, 1)

    def on_dve(self, dve, psum):
        dve.wait_ge(self.abs1, KH)
        dve.wait_ge(self.loaded, 48)
        dve.tensor_scalar(self.a1[:], self.a1[:], 1.0 / D, None, ALU.mult).then_inc(self.ready, 1)
        dve.tensor_scalar(self.b2[:], self.b2[:], 0.5, None, ALU.mult).then_inc(self.ready, 1)
        dve.wait_ge(self.sum2, 1)
        dve.tensor_scalar(self.a2[:], psum, 0.5 / H, None, ALU.mult).then_inc(self.ready, 1)
        dve.wait_ge(self.ready, 3)


class RowNorm:

    STEPS = 3 * G + 1 - G

    def __init__(self, nc, ctx, tag, eps, mhalf, consts):
        self.st = ctx.enter_context(nc.sbuf_tensor(f"{tag}_st", [P, G, 6], F32))
        self.mv = ctx.enter_context(nc.sbuf_tensor(f"{tag}_mv", [P, G, 2], F32))
        self.ve = ctx.enter_context(nc.sbuf_tensor(f"{tag}_ve", [P, G], F32))
        self.rs = ctx.enter_context(nc.sbuf_tensor(f"{tag}_rs", [P, G], F32))
        self.var_ready = ctx.enter_context(nc.semaphore(f"{tag}_var_ready"))
        self.rstd_ready = ctx.enter_context(nc.semaphore(f"{tag}_rstd_ready"))
        self.eps, self.mhalf, self.consts = eps, mhalf, consts

    def stats(self, dve, ch, src, i):
        for g in range(G):
            ch.add(dve.bn_stats(self.st[:, g, :], src[:, g, :]))
        hold(dve, (self.consts, 1), ch.sem, ch.base + ch.n)
        for g in range(G):
            ch.add(dve.bn_aggr(self.mv[:, g, :], self.st[:, g, :]))
        ch.sync()
        dve.tensor_scalar(self.ve[:], self.mv[:, :, 1], self.eps, None, ALU.add).then_inc(self.var_ready, 1)

    def on_pool(self, pool, i):
        pool.wait_ge(self.var_ready, i + 1)
        pool.tensor_tensor(self.rs[:], self.ve[:], self.mhalf, ALU.pow).then_inc(self.rstd_ready, 1)

    def apply(self, dve, src, dst, i, done):
        dve.wait_ge(self.rstd_ready, i + 1)
        for g in range(G):
            dve.tensor_scalar(dst[:, g, :], src[:, g, :], self.mv[:, g, 0:1], self.rs[:, g:g + 1],
                              ALU.subtract, ALU.mult).then_inc(done, 1)


class Ffn:

    DVE_STEPS = 2 * G

    def __init__(self, nc, ctx, tag, w, psT, psM, psO):
        def sb(name, shape):
            return ctx.enter_context(nc.sbuf_tensor(f"{tag}_{name}", shape, F32))

        def sem(name):
            return ctx.enter_context(nc.semaphore(f"{tag}_{name}"))

        self.w, self.psT, self.psM, self.psO = w, psT, psM, psO
        self.xn = sb("xn", [P, G, D])
        self.xb = sb("xb", [P, G, D])
        self.xT = sb("xT", [P, KD, COLS])
        self.g = sb("g", [P, KH, COLS])
        self.norm = RowNorm(nc, ctx, f"{tag}_ln", 1e-5, w.mhalf[:], w.consts)
        self.chain = sem("dve_chain")
        self.kept = sem("kept")
        self.xn_ready = sem("xn_ready")
        self.xb_ready = sem("xb_ready")
        self.turned = sem("turned")
        self.xT_ready = sem("xT_ready")
        self.up_done = sem("up_done")
        self.gelu_done = sem("gelu_done")
        self.down_done = sem("down_done")
        self.scaled = sem("scaled")
        self.dst_ready = sem("dst_ready")

    def primed(self):
        return [self.turned, self.down_done, self.scaled, self.chain, self.xn_ready, self.kept,
                self.dst_ready]

    def dve_in(self, dve, src, i):
        ch = Chain(dve, self.chain, self.DVE_STEPS, i)
        self.norm.stats(dve, ch, src, i)
        dve.wait_ge(self.turned, FIRST + i * KD)
        self.norm.apply(dve, src, self.xn, i, self.xn_ready)

    def dve_keep(self, dve, src, i):
        dve.tensor_tensor(self.xb[:], src[:], self.w.b2[:].unsqueeze(1).broadcast_to([P, G, D]),
                          ALU.add).then_inc(self.kept, 1)

    def pe_in(self, pe, i):
        pe.wait_ge(self.xn_ready, FIRST + i * G + G)
        for k in range(KD):
            for g in range(G):
                mm = pe.transpose(self.psT[:, k, g * P:(g + 1) * P], self.xn[:, g, k * P:(k + 1) * P],
                                  self.w.ident[:])
            mm.then_inc(self.turned, 1)

    def act_in(self, act, i):
        for k in range(KD):
            act.wait_ge(self.turned, FIRST + i * KD + k + 1)
            act.activation(self.xT[:, k, :], self.psT[:, k, :], ACT.Copy).then_inc(self.xT_ready, 1)

    def pe_up(self, pe, i):
        pe.wait_ge(self.xT_ready, i * KD + KD)
        for m in range(KH):
            if m >= 2:
                pe.wait_ge(self.gelu_done, i * KH + m - 1)
            for k in range(KD):
                mm = pe.matmul(self.psM[:, m % 2, :], self.w.s1[:, k, m * P:(m + 1) * P], self.xT[:, k, :],
                               start=(k == 0), stop=(k == KD - 1))
            mm.then_inc(self.up_done, 1)

    def act_up(self, act, i):
        for m in range(KH):
            act.wait_ge(self.up_done, i * KH + m + 1)
            if m == 0:
                act.wait_ge(self.down_done, FIRST + i)
            act.activation(self.g[:, m, :], self.psM[:, m % 2, :], ACT.Gelu, bias=self.w.b1[:, m:m + 1],
                           scale=self.w.a1[:, m:m + 1]).then_inc(self.gelu_done, 1)

    def pe_down(self, pe, i, g0=0, g1=G):
        if g0 == 0:
            pe.wait_ge(self.gelu_done, i * KH + KH)
            pe.wait_ge(self.scaled, FIRST + i)
        for g in range(g0, g1):
            for k in range(KH):
                mm = pe.matmul(self.psO[:, g, :], self.g[:, k, g * P:(g + 1) * P], self.w.s2[:, k, :],
                               start=(k == 0), stop=(k == KH - 1))
        if g1 == G:
            mm.then_inc(self.down_done, 1)

    def dve_out(self, dve, dst, i):
        dve.wait_ge(self.down_done, FIRST + i + 1)
        dve.tensor_tensor(dst[:], self.psO[:], self.w.a2[:].unsqueeze(1).broadcast_to([P, G, D]),
                          ALU.mult).then_inc(self.scaled, 1)
        dve.wait_ge(self.scaled, FIRST + i + 1)
        dve.wait_ge(self.kept, FIRST + i + 1)
        dve.tensor_tensor(dst[:], dst[:], self.xb[:], ALU.add).then_inc(self.dst_ready, 1)


def pre_stage(nc, dram):
    with ExitStack() as ctx:
        def sb(name, shape):
            return ctx.enter_context(nc.sbuf_tensor(name, shape, F32))

        def sem(name):
            return ctx.enter_context(nc.semaphore(name))

        psT = ctx.enter_context(nc.psum_tensor("p_psT", [P, KD, COLS], F32))
        psM = ctx.enter_context(nc.psum_tensor("p_psM", [P, 2, COLS], F32))
        psB = ctx.enter_context(nc.psum_tensor("p_psB", [P, 2, COLS], F32))
        psO = ctx.enter_context(nc.psum_tensor("p_psO", [P, G, D], F32))
        w = FfnWeights(nc, ctx, dram, "fa")
        ffn = Ffn(nc, ctx, "fa", w, psT, psM, psO)
        ln2 = RowNorm(nc, ctx, "ln2", 1e-5, w.mhalf[:], w.consts)

        win = sb("win", [P, KD, 2 * E])
        wdt = sb("wdt", [P, KE, E])
        wbc = sb("wbc", [P, KE, 2 * N])
        convw = sb("convw", [P, KE, TAPS])
        convb = sb("convb", [P, KE])
        bdt = sb("bdt", [P, KE])
        normw = sb("normw", [P, KD])
        dtbias = sb("dtbias", [P, 1])
        xt = sb("xt", [P, G, D])
        x1 = sb("x1", [P, G, D])
        z = sb("z", [P, G, D])
        r = sb("r", [P, G, D])
        zn = sb("zn", [P, G, D])
        sq = sb("sq", [P, G, D])
        ss = sb("ss", [P, G])
        v2 = sb("v2", [P, G])
        rr = sb("rr", [P, G])
        zT = sb("zT", [P, KD, COLS])
        xbuf = sb("xbuf", [P, KE, B, TAPS - 1 + TT])
        sg = sb("sg", [P, KE, COLS])
        cv = sb("cv", [P, KE, COLS])
        xc = sb("xc", [P, KE, COLS])
        v = sb("v", [P, KE, COLS])
        e = sb("e", [P, KE, COLS])
        dt = sb("dt", [P, KE, COLS])
        u = sb("u", [P, KE, COLS])
        bcs = sb("bcs", [2 * N, COLS])
        w1n = u[:].rearrange("p a (c k) -> p (a c) k", k=D)
        w2abs = v[:].rearrange("p a (c k) -> p (a c) k", k=D)
        pad = cv

        p_loaded = sem("p_loaded")
        bias_set = sem("bias_set")
        padded = sem("padded")
        pad_zero = sem("pad_zero")
        x_in = sem("x_in")
        z_ready = sem("z_ready")
        r_ready = sem("r_ready")
        ms_ready = sem("ms_ready")
        rms_ready = sem("rms_ready")
        zn_ready = sem("zn_ready")
        z_turned = sem("z_turned")
        zT_ready = sem("zT_ready")
        proj_done = sem("proj_done")
        proj_read = sem("proj_read")
        conv_done = sem("conv_done")
        halo_done = sem("halo_done")
        xc_ready = sem("xc_ready")
        act_chain = sem("act_chain")
        dve_chain = sem("p_dve_chain")
        sp_ready = sem("sp_ready")
        th_ready = sem("th_ready")
        l_ready = sem("l_ready")
        dt_ready = sem("dt_ready")
        u_ready = sem("u_ready")
        r_out, sg_out, xc_out, bc_out, dt_out, u_out = (
            sem(n) for n in ("r_out", "sg_out", "xc_out", "bc_out", "dt_out", "u_out"))

        prime(nc, ffn.primed() + [zT_ready, proj_read, sg_out, xc_out, r_ready, u_ready, dt_ready, bc_out, r_out, z_turned,
                                  xc_ready, dt_out, u_out, act_chain, dve_chain])
        DVE_B = 2 * G + G + (TAPS - 1) * KE + 1
        ACT_B = 2
        NP = 2 * KE + KE + 1

        def steps(i):
            return bass.ds(i * TT, TT)

        with nc.Block() as block:
            @block.sync
            def _(sp):
                def load_x(i):
                    hold(sp, (w.loaded, 48), ffn.xn_ready, FIRST + i * G)
                    hold(sp, (w.loaded, 48), ffn.kept, FIRST + i)
                    for b in range(B):
                        sp.dma_start(xt[:, 2 * b:2 * b + 2, :],
                                     dram["x"][b, steps(i), :].rearrange("(h p) d -> p h d", p=P)
                                     ).then_inc(x_in, 16)

                w.load(sp, w1n)
                load_x(0)
                for dst, src in ((win[:], dram["winT"].rearrange("(k p) m -> p k m", p=P)),
                                 (wdt[:], dram["wdtT"].rearrange("(k p) m -> p k m", p=P)),
                                 (wbc[:], dram["wbcT"].rearrange("(k p) m -> p k m", p=P)),
                                 (convw[:], dram["convw"]), (convb[:], dram["convb"]),
                                 (bdt[:], dram["bdt"]), (normw[:], dram["normw"])):
                    sp.dma_start(dst, src).then_inc(p_loaded, 16)
                sp.wait_ge(pad_zero, 1)
                n = LP - L
                zero = pad[:].rearrange("p a c -> p (a c)")[:, 0:KE * B * n].rearrange("p (a c) -> p a c", c=n)
                sp.dma_start(dram["dt"][:, :, L:LP], zero).then_inc(padded, 16)
                sp.dma_start(dram["u"][:, :, L:LP], zero).then_inc(padded, 16)
                sp.dma_start(dram["bc"][:, :, L:LP], zero[0:2 * N, 0:B, :]).then_inc(padded, 16)
                def store(name, tile, done, i):
                    sp.dma_start(dram[name][:, :, steps(i)],
                                 tile.rearrange("p a (b t) -> p (a b) t", b=B)).then_inc(done, 16)

                def body(i, ahead):
                    if ahead == 2:
                        load_x(i + 2)
                    hold(sp, (w.loaded, 48), r_ready, FIRST + i + 1)
                    for b in range(B):
                        sp.dma_start(dram["r"][b, steps(i), :].rearrange("(h p) d -> p h d", p=P),
                                     r[:, 2 * b:2 * b + 2, :]).then_inc(r_out, 16)
                    hold(sp, (w.loaded, 48), proj_read, FIRST + i * NP + 2 * KE)
                    store("sg", sg[:], sg_out, i)
                    hold(sp, (w.loaded, 48), xc_ready, FIRST + i + 1)
                    store("xc", xc[:], xc_out, i)
                    hold(sp, (w.loaded, 48), proj_read, FIRST + i * NP + NP)
                    sp.dma_start(dram["bc"][:, :, steps(i)],
                                 bcs[:].rearrange("p (b t) -> p b t", b=B)).then_inc(bc_out, 16)
                    hold(sp, (w.loaded, 48), dt_ready, FIRST + i + 1)
                    store("dt", dt[:], dt_out, i)
                    hold(sp, (w.loaded, 48), u_ready, FIRST + i + 1)
                    store("u", u[:], u_out, i)

                load_x(1)
                with sp.Fori(0, TILES - 2) as i:
                    body(i, 2)
                body(TILES - 2, 1)
                body(TILES - 1, 0)
                sp.wait_ge(padded, 48)
                for s, n in ((r_out, 32), (sg_out, 16), (xc_out, 16), (bc_out, 16), (dt_out, 16), (u_out, 16)):
                    sp.wait_ge(s, FIRST + n * TILES)

            @block.gpsimd
            def _(pool):
                w.on_pool(pool)

                def body(i, ahead):
                    ln2.on_pool(pool, i)
                    pool.wait_ge(ms_ready, i + 1)
                    pool.tensor_tensor(rr[:], v2[:], w.mhalf[:], ALU.pow).then_inc(rms_ready, 1)
                    if ahead == 2:
                        ffn.norm.on_pool(pool, i + 2)

                ffn.norm.on_pool(pool, 0)
                ffn.norm.on_pool(pool, 1)
                with pool.Fori(0, TILES - 2) as i:
                    body(i, 2)
                body(TILES - 2, 1)
                body(TILES - 1, 0)

            @block.tensor
            def _(pe):
                w.on_pe(pe, w2abs, psO[:, 0, :])
                pe.wait_ge(w.signs, 2)
                pe.wait_ge(w.ready, 3)

                def body(i, ahead):
                    if ahead:
                        pe.wait_ge(zT_ready, FIRST + i * KD)
                        ffn.pe_in(pe, i + 1)
                        ffn.pe_up(pe, i + 1)
                    pe.wait_ge(zn_ready, i * G + G)
                    for k in range(KD):
                        for g in range(G):
                            mm = pe.transpose(psT[:, k, g * P:(g + 1) * P], zn[:, g, k * P:(k + 1) * P],
                                              w.ident[:])
                        mm.then_inc(z_turned, 1)
                    pe.wait_ge(zT_ready, FIRST + i * KD + KD)
                    for m in range(2 * KE):
                        pe.wait_ge(proj_read, FIRST + (i * NP + m - 1 if m >= 2 else i * NP))
                        for k in range(KD):
                            mm = pe.matmul(psB[:, m % 2, :], win[:, k, m * P:(m + 1) * P], zT[:, k, :],
                                           start=(k == 0), stop=(k == KD - 1))
                        mm.then_inc(proj_done, 1)
                    if ahead:
                        ffn.pe_down(pe, i + 1, 0, SPLIT)
                    pe.wait_ge(xc_ready, FIRST + i + 1)
                    for m in range(KE):
                        pe.wait_ge(proj_read, FIRST + i * NP + 2 * KE + m - 1)
                        for k in range(KE):
                            mm = pe.matmul(psB[:, m % 2, :], wdt[:, k, m * P:(m + 1) * P], xc[:, k, :],
                                           start=(k == 0), stop=(k == KE - 1))
                        mm.then_inc(proj_done, 1)
                    pe.wait_ge(proj_read, FIRST + i * NP + 3 * KE - 1)
                    for k in range(KE):
                        mm = pe.matmul(psB[0:2 * N, 0, :], wbc[:, k, :], xc[:, k, :],
                                       start=(k == 0), stop=(k == KE - 1))
                    mm.then_inc(proj_done, 1)
                    if ahead:
                        ffn.pe_down(pe, i + 1, SPLIT, G)

                ffn.pe_in(pe, 0)
                ffn.pe_up(pe, 0)
                ffn.pe_down(pe, 0)
                pe.wait_ge(p_loaded, 16 * 7)
                with pe.Fori(0, TILES - 2) as i:
                    body(i, 2)
                body(TILES - 2, 1)
                body(TILES - 1, 0)

            @block.scalar
            def _(act):
                w.on_act(act, w1n, w2abs)
                act.wait_ge(w.ready, 3)
                def body(i, ahead):
                    ch = Chain(act, act_chain, ACT_B, i)
                    if ahead:
                        ffn.act_up(act, i + 1)
                    for k in range(KD):
                        act.wait_ge(z_turned, FIRST + i * KD + k + 1)
                        act.activation(zT[:, k, :], psT[:, k, :], ACT.Copy,
                                       scale=normw[:, k:k + 1]).then_inc(zT_ready, 1)
                    act.wait_ge(halo_done, i + 1)
                    act.wait_ge(sg_out, FIRST + i * 16)
                    for m in range(2 * KE):
                        act.wait_ge(proj_done, i * NP + m + 1)
                        if m < KE:
                            act.activation(xbuf[:, m, :, TAPS - 1:], psB[:, m % 2, :].rearrange("p (b t) -> p b t", b=B),
                                           ACT.Copy).then_inc(proj_read, 1)
                        else:
                            act.activation(sg[:, m - KE, :], psB[:, m % 2, :], ACT.Silu).then_inc(proj_read, 1)
                    act.wait_ge(conv_done, i * KE + KE)
                    act.wait_ge(xc_out, FIRST + i * 16)
                    act.wait_ge(u_ready, FIRST + i)
                    act.activation(xc[:], cv[:], ACT.Silu).then_inc(xc_ready, 1)
                    for m in range(KE):
                        act.wait_ge(proj_done, i * NP + 2 * KE + m + 1)
                        act.activation(v[:, m, :], psB[:, m % 2, :], ACT.Identity,
                                       bias=bdt[:, m:m + 1]).then_inc(proj_read, 1)
                    act.wait_ge(proj_done, i * NP + NP)
                    act.wait_ge(bc_out, FIRST + i * 16)
                    act.activation(bcs[:], psB[0:2 * N, 0, :], ACT.Copy).then_inc(proj_read, 1)
                    act.wait_ge(proj_read, FIRST + i * NP + NP - 1)
                    act.wait_ge(dt_ready, FIRST + i)
                    ch.add(act.activation(e[:], v[:], ACT.Abs))
                    ch.sync()
                    ch.add(act.activation(e[:], e[:], ACT.Exp, scale=-1.0))
                    ch.sync()
                    act.activation(e[:], e[:], ACT.Ln, bias=w.ones[:, 0:1]).then_inc(l_ready, 1)
                    if ahead == 2:
                        ffn.act_in(act, i + 2)
                    act.wait_ge(sp_ready, i + 1)
                    act.activation(e[:], v[:], ACT.Tanh, scale=SHARP / (DT_HALF + 1e-8),
                                   bias=dtbias[:]).then_inc(th_ready, 1)
                    ch.done()

                ffn.act_in(act, 0)
                ffn.act_up(act, 0)
                ffn.act_in(act, 1)
                act.wait_ge(p_loaded, 16 * 7)
                act.wait_ge(bias_set, 1)
                with act.Fori(0, TILES - 2) as i:
                    body(i, 2)
                body(TILES - 2, 1)
                body(TILES - 1, 0)

            @block.vector
            def _(dve):
                dve.memset(pad[:], 0.0).then_inc(pad_zero, 1)
                dve.memset(xbuf[:, :, :, 0:TAPS - 1], 0.0).then_inc(halo_done, 1)
                dve.memset(dtbias[:], -DT_MID * SHARP / (DT_HALF + 1e-8)).then_inc(bias_set, 1)

                def feed(i):
                    dve.wait_ge(x_in, i * 32 + 32)
                    ffn.dve_in(dve, xt, i)

                def body(i, ahead):
                    ch = Chain(dve, dve_chain, DVE_B, i)
                    dve.wait_ge(ffn.dst_ready, FIRST + i + 1)
                    ln2.stats(dve, ch, x1, i)
                    ln2.apply(dve, x1, z, i, z_ready)
                    dve.wait_ge(z_ready, i * G + G)
                    for g in range(G):
                        ch.add(dve.tensor_tensor_reduce(out=sq[:, g, :], in0=z[:, g, :], in1=z[:, g, :], scale=1.0,
                                                        scalar=0.0, op0=ALU.mult, op1=ALU.add,
                                                        accum_out=ss[:, g:g + 1]))
                    ch.sync()
                    dve.tensor_scalar(v2[:], ss[:], 1.0 / D, 1e-6, ALU.mult, ALU.add).then_inc(ms_ready, 1)
                    dve.wait_ge(r_out, FIRST + i * 32)
                    dve.tensor_tensor(r[:], x1[:], z[:], ALU.add).then_inc(r_ready, 1)
                    dve.wait_ge(rms_ready, i + 1)
                    dve.wait_ge(z_turned, FIRST + i * KD)
                    for g in range(G):
                        dve.tensor_scalar(zn[:, g, :], z[:, g, :], rr[:, g:g + 1], None,
                                          ALU.mult).then_inc(zn_ready, 1)
                    dve.wait_ge(proj_read, FIRST + i * NP + KE)
                    dve.wait_ge(xc_ready, FIRST + i)
                    for tap in range(TAPS):
                        for c in range(KE):
                            out = cv[:, c, :].rearrange("p (b t) -> p b t", b=B)
                            src = xbuf[:, c, :, tap:tap + TT]
                            if tap == 0:
                                ins = dve.tensor_scalar(out, src, convw[:, c, 0:1], convb[:, c:c + 1],
                                                        ALU.mult, ALU.add)
                            else:
                                ins = dve.scalar_tensor_tensor(out=out, in0=src, scalar=convw[:, c, tap:tap + 1],
                                                               in1=out, op0=ALU.mult, op1=ALU.add)
                            if tap == TAPS - 1:
                                ins.then_inc(conv_done, 1)
                            else:
                                ch.add(ins)
                        if tap < TAPS - 1:
                            ch.sync()
                    dve.wait_ge(conv_done, i * KE + KE)
                    ch.add(dve.tensor_copy(sq[:, 0, 0:KE * B * (TAPS - 1)].rearrange("p (c b t) -> p c b t", c=KE, b=B),
                                           xbuf[:, :, :, TT:]))
                    ch.sync()
                    dve.tensor_copy(xbuf[:, :, :, 0:TAPS - 1],
                                    sq[:, 0, 0:KE * B * (TAPS - 1)].rearrange("p (c b t) -> p c b t", c=KE, b=B)
                                    ).then_inc(halo_done, 1)
                    dve.wait_ge(halo_done, i + 2)
                    if ahead:
                        if ahead == 2:
                            feed(i + 2)
                        dve.wait_ge(r_ready, FIRST + i + 1)
                        ffn.dve_out(dve, x1, i + 1)
                        if ahead == 2:
                            dve.wait_ge(ffn.dst_ready, FIRST + i + 2)
                            ffn.dve_keep(dve, xt, i + 2)
                    dve.wait_ge(l_ready, i + 1)
                    dve.scalar_tensor_tensor(out=v[:], in0=v[:], scalar=0.0, in1=e[:], op0=ALU.max,
                                             op1=ALU.add).then_inc(sp_ready, 1)
                    dve.wait_ge(th_ready, i + 1)
                    dve.wait_ge(dt_out, FIRST + i * 16)
                    dve.tensor_scalar(dt[:], e[:], DT_HALF / SHARP, DT_MID, ALU.mult, ALU.add).then_inc(dt_ready, 1)
                    dve.wait_ge(dt_ready, FIRST + i + 1)
                    dve.wait_ge(u_out, FIRST + i * 16)
                    dve.tensor_tensor(u[:], dt[:], xc[:], ALU.mult).then_inc(u_ready, 1)
                    ch.done()

                feed(0)
                w.on_dve(dve, psO[:, 0, :])
                ffn.dve_keep(dve, xt, 0)
                feed(1)
                ffn.dve_out(dve, x1, 0)
                dve.wait_ge(ffn.dst_ready, FIRST + 1)
                ffn.dve_keep(dve, xt, 1)
                dve.wait_ge(p_loaded, 16 * 7)
                dve.wait_ge(padded, 48)
                with dve.Fori(0, TILES - 2) as i:
                    body(i, 2)
                body(TILES - 2, 1)
                body(TILES - 1, 0)


def scan_stage(nc, dram):
    with ExitStack() as ctx:
        def sb(name, shape):
            return ctx.enter_context(nc.sbuf_tensor(name, shape, F32))

        def sem(name):
            return ctx.enter_context(nc.semaphore(name))

        decay = sb("decay", [P, 2, CB, ROWS * W])
        dtc = sb("dtc", [P, 2, KE * B, CT])
        uc = [sb(f"uc{h}", [P, KE * B, HALF]) for h in range(2)]
        bc = [sb(f"bc{q}", [P, 2, B * N, S]) for q in range(3)]
        inp = sb("inp", [P, ROWS, W])
        h = sb("h", [P, ROWS, W])
        hc = sb("hc", [P, 2, ROWS, 2 * S])
        yc = sb("yc", [P, 2, KE * B, CT])
        a16 = sb("a16", [P, KE * N])
        ones = sb("sc_ones", [P, P])
        ident = sb("sc_ident", [P, P])
        sq = sb("sc_sq", [P, B, KE * N])
        ss = sb("sc_ss", [P, B])
        qs = sb("qs", [P, B])
        rc = sb("rc", [P, B])
        mhalf = sb("mhalf", [P, B])
        u0 = sb("u0", [P, KE * B, 2])
        b0 = sb("b0", [P, B, N, 2])
        psQ = ctx.enter_context(nc.psum_tensor("psQ", [P, 512], F32))
        psY = ctx.enter_context(nc.psum_tensor("psY", [P, 2, 512], F32))

        s_in = sem("s_in")
        dt_in = [sem(f"dt_in{q}") for q in range(2)]
        u_in = [sem(f"u_in{q}") for q in range(2)]
        bc_in = [sem(f"bc_in{q}") for q in range(3)]
        blk_out = sem("blk_out")
        consts = sem("s_consts")
        filled = sem("s_filled")
        zeroed = sem("s_zeroed")
        a_steps = sem("a_steps")
        tanh_done = sem("tanh_done")
        decay_ready = sem("decay_ready")
        inp_ready = sem("inp_ready")
        carry_ready = sem("carry_ready")
        h_ready = sem("h_ready")
        sq_ready = sem("sq_ready")
        sum_ready = sem("sum_ready")
        sum_copied = sem("sum_copied")
        norm_ready = sem("norm_ready")
        hc_ready = sem("hc_ready")
        y_summed = sem("y_summed")
        y_copied = sem("y_copied")
        y_out = [sem(f"y_out{q}") for q in range(2)]

        prime(nc, [inp_ready, hc_ready, carry_ready, sum_copied, *y_out], [y_copied, y_summed])

        def rows(ap):
            return ap.rearrange("p (c b n) e -> p c b n e", c=KE, b=B)

        drow = decay[:].rearrange("p q k (c b n e) -> p q k c b n e", c=KE, b=B, e=W)

        NCH = KE * N
        cut = [round(q * NCH / CB) for q in range(CB + 1)]

        with nc.Block() as block:
            @block.sync
            def _(sp):
                sp.dma_start(a16[:], dram["alog"]).then_inc(s_in, 16)
                sp.dma_start(u0[:], dram["u"][:, :, 0:2]).then_inc(s_in, 16)
                for b in range(B):
                    sp.dma_start(b0[:, b], dram["bc"][0:N, b:b + 1, 0:2].rearrange("n b t -> b n t")
                                 .broadcast_to([P, N, 2])).then_inc(s_in, 16)

                def relayout(c):
                    for q in range(2):
                        for b in range(B):
                            sp.dma_start(
                                dram["blk"][bass.ds(c * CB, CB), q, b, :, :].rearrange("k n t -> n k t"),
                                dram["bc"][q * N:(q + 1) * N, b, bass.ds(c * CT + 1 - q, CT)]
                                .rearrange("n (k t) -> n k t", t=S)).then_inc(blk_out, 16)

                def load_dt(c, q):
                    sp.dma_start(dtc[:, q], dram["dt"][:, :, bass.ds(c * CT + 1, CT)]).then_inc(dt_in[q], 16)

                def load_u(c, half):
                    sp.dma_start(uc[half][:], dram["u"][:, :, bass.ds(c * CT + 1 + half * HALF, HALF)]
                                 ).then_inc(u_in[half], 16)

                def load_bc(j, q):
                    sp.dma_start(bc[q][:], dram["blk"][bass.ds(j, 1)].rearrange("o q b n t -> o (q b n t)")
                                 .broadcast_to([P, 2 * B * N * S])).then_inc(bc_in[q], 16)

                def store_y(c, q, pairs, copied):
                    hold(sp, (s_in, 64), y_copied, BUFS + copied)
                    sp.dma_start(dram["y"][:, :, bass.ds(c * CT, pairs * 2 * S)],
                                 yc[:, q, :, 0:pairs * 2 * S]).then_inc(y_out[q], 16)

                load_dt(0, 0)
                relayout(0)
                load_u(0, 0)
                sp.wait_ge(blk_out, 64)
                load_bc(0, 0)
                load_bc(1, 1)
                load_dt(1, 1)

                def turn(t, first, slots, tail=False):
                    j0 = t * BODY
                    for s in range(first, slots):
                        c, cs, q = t * 2 + s // CB, s % CB, s // CB % 2
                        more = not tail or s // CB == 0
                        if cs == 0:
                            hold(sp, (s_in, 64), inp_ready, FIRST + c * CB)
                            load_u(c, 1)
                            if more:
                                relayout(c + 1)
                            if not tail:
                                hold(sp, (s_in, 64), tanh_done, c * NCH + NCH)
                                load_dt(c + 2, q)
                        if cs == 6 and more:
                            hold(sp, (s_in, 64), inp_ready, FIRST + c * CB + 6)
                            load_u(c + 1, 0)
                        if not tail or s + 2 < slots:
                            if cs == CB - 2:
                                hold(sp, (s_in, 64), blk_out, c * 64 + 128)
                            hold(sp, (s_in, 64), hc_ready, FIRST + j0 + s)
                            load_bc(j0 + s + 2, (s + 2) % 3)
                        if s == 14 and not tail:
                            store_y(t * 2, 0, PAIRS_BODY // 2, t * PAIRS_BODY + PAIRS_BODY // 2)
                        if s == BODY + 2:
                            store_y(t * 2 + 1, 1, PAIRS_BODY // 2, t * PAIRS_BODY + PAIRS_BODY)
                turn(0, 0, 3)
                with sp.Fori(0, TURNS) as t:
                    turn(t, 3, BODY + 3)
                turn(TURNS, 3, TAIL, tail=True)
                half = PAIRS_BODY // 2
                store_y(TURNS * 2, 0, half, TURNS * PAIRS_BODY + half)
                store_y(TURNS * 2 + 1, 1, TAIL // 2 - half, TURNS * PAIRS_BODY + TAIL // 2)
                for q in range(2):
                    sp.wait_ge(y_out[q], FIRST + 16 * (TURNS + 1))

            @block.gpsimd
            def _(pool):
                pool.memset(ident[:], 0.0).then_inc(filled, 1)
                pool.memset(ones[:], 1.0 / CLAMP ** 2).then_inc(filled, 1)
                pool.memset(mhalf[:], -0.5).then_inc(filled, 1)
                pool.wait_ge(filled, 3)
                pool.affine_select(out=ident[:], in_=ident[:], compare_op=ALU.not_equal, fill=1.0,
                                   base=0, pattern=[[-1, P]], channel_multiplier=1).then_inc(consts, 1)
                with pool.Fori(0, TURNS * BODY + TAIL) as c:
                    pool.wait_ge(sum_copied, FIRST + c + 1)
                    pool.wait_ge(decay_ready, c + 1)
                    pool.wait_ge(carry_ready, FIRST + c)
                    pool.tensor_tensor(rc[:], qs[:], mhalf[:], ALU.pow).then_inc(norm_ready, 1)

            @block.tensor
            def _(pe):
                pe.wait_ge(consts, 1)

                def total(c):
                    pe.wait_ge(sq_ready, c * B + B)
                    pe.wait_ge(sum_copied, FIRST + c)
                    pe.matmul(psQ[:, 0:B], ones[:], ss[:], start=True, stop=True).then_inc(sum_ready, 1)

                def readout(p, pl, n0, n1):
                    if n0 == 0:
                        pe.wait_ge(hc_ready, FIRST + p * 2 + 2)
                        pe.wait_ge(y_copied, p + 1)
                    for n in range(n0, n1):
                        rhs = hc[:, pl % 2].rearrange("p (c n) t -> p c n t", n=N)[:, :, n, :]
                        mm = pe.matmul(psY[:, pl % 2, 0:KE * B * 2 * S], ident[:], rhs,
                                       start=(n == 0), stop=(n == N - 1))
                    if n1 == N:
                        mm.then_inc(y_summed, 1)

                def turn(t, first, slots, tail=False):
                    for s in range(first, slots):
                        if not (tail and s == slots - 1):
                            total(t * BODY + s + 1)
                        if s % 2 == 0 and s > 0:
                            readout(t * 12 + s // 2 - 1, s // 2 - 1, N // 2, N)
                        if s % 2 == 1:
                            last = tail and s == slots - 1
                            readout(t * 12 + s // 2, s // 2, 0, N if last else N // 2)
                total(0)
                turn(0, 0, 1)
                with pe.Fori(0, TURNS) as t:
                    turn(t, 1, BODY + 1)
                turn(TURNS, 1, TAIL, tail=True)

            @block.scalar
            def _(act):
                act.wait_ge(s_in, 64)
                act.activation(a16[:], a16[:], ACT.Tanh, scale=SHARP / (A_HALF + 1e-8)).then_inc(a_steps, 1)
                act.wait_ge(a_steps, 1)
                act.activation(a16[:], a16[:], ACT.Exp, scale=A_HALF / SHARP).then_inc(a_steps, 1)
                act.wait_ge(a_steps, 3)

                def squares(c):
                    act.wait_ge(h_ready, c + 1)
                    for b in range(B):
                        act.activation(sq[:, b, :].rearrange("p (c n) -> p c n", c=KE), rows(h[:])[:, :, b, :, S],
                                       ACT.Square, accum_out=ss[:, b:b + 1]).then_inc(sq_ready, 1)

                def tanhs(c, q, lo, hi, blocks=CB):
                    for m in range(lo, hi):
                        k, n = m // N, m % N
                        act.activation(drow[:, q, 0:blocks, k, :, n, 1:].rearrange("p k b e -> p b k e"),
                                       dtc[:, q, k * B:(k + 1) * B, 0:blocks * S].rearrange("p b (k e) -> p b k e", e=S),
                                       ACT.Tanh, scale=a16[:, m:m + 1]).then_inc(tanh_done, 1)

                def decays(q, k):
                    ap = decay[:, q, k, :].rearrange("p (r e) -> p r e", e=W)[:, :, 1:]
                    act.activation(ap, ap, ACT.Exp, scale=DTA_HALF / SHARP).then_inc(decay_ready, 1)

                def copy_y(t, pl):
                    half, o = pl // 6, pl % 6 * 2 * S
                    if pl % 6 == 0:
                        act.wait_ge(y_out[half], FIRST + t * 16)
                    act.wait_ge(y_summed, BUFS + t * PAIRS_BODY + pl + 1)
                    act.activation(yc[:, half, :, o:o + 2 * S],
                                   psY[:, pl % 2, 0:KE * B * 2 * S].rearrange("p (c t) -> p c t", t=2 * S),
                                   ACT.Copy).then_inc(y_copied, 1)

                squares(0)
                act.wait_ge(dt_in[0], 16)
                tanhs(0, 0, 0, NCH)
                act.wait_ge(tanh_done, NCH)
                decays(0, 0)

                def turn(t, first, slots, tail=False):
                    for s in range(first, slots):
                        c, cs, q = t * 2 + s // CB, s % CB, s // CB % 2
                        more = not tail or s // CB == 0
                        if not (tail and s == slots - 1):
                            squares(t * BODY + s + 1)
                        if cs < CB - 1 and not (tail and s == slots - 1):
                            decays(q, cs + 1)
                        if s % 2 == 1 and s >= 3:
                            copy_y(t, s // 2 - 1)
                        if cs == 0 and more:
                            act.wait_ge(dt_in[1 - q], (t + s // BODY) * 16 + 16 + q * 16)
                            act.wait_ge(h_ready, c * CB + 1)
                        if more:
                            tanhs(c + 1, 1 - q, cut[cs], cut[cs + 1], TAIL - CB if tail else CB)
                        if cs == CB - 1:
                            act.wait_ge(tanh_done, c * NCH + 2 * NCH)
                            decays(1 - q, 0)
                turn(0, 0, 2)
                with act.Fori(0, TURNS) as t:
                    turn(t, 2, BODY + 2)
                turn(TURNS, 2, TAIL, tail=True)
                copy_y(TURNS, TAIL // 2 - 1)

            @block.vector
            def _(dve):
                dve.memset(decay[:, 0].rearrange("p k (r e) -> p k r e", e=W)[:, :, :, 0], 0.0).then_inc(zeroed, 1)
                dve.memset(decay[:, 1].rearrange("p k (r e) -> p k r e", e=W)[:, :, :, 0], 0.0).then_inc(zeroed, 1)
                dve.wait_ge(a_steps, 2)
                dve.tensor_scalar(a16[:], a16[:], -SHARP / (DTA_HALF + 1e-8), None, ALU.mult).then_inc(a_steps, 1)
                dve.wait_ge(zeroed, 2)
                dve.wait_ge(filled, 3)

                dve.wait_ge(s_in, 64)
                dve.tensor_tensor(
                    h[:, :, S].rearrange("p (c b n) -> p c b n", c=KE, b=B),
                    u0[:, :, 0].rearrange("p (c b) -> p c b", b=B).unsqueeze(3).broadcast_to([P, KE, B, N]),
                    b0[:, :, :, 0].unsqueeze(1).broadcast_to([P, KE, B, N]),
                    ALU.mult).then_inc(h_ready, 1)

                def copy_sum(c):
                    dve.wait_ge(sum_ready, c + 1)
                    dve.tensor_scalar(qs[:], psQ[:, 0:B], 1.0, None, ALU.max).then_inc(sum_copied, 1)

                def inputs(k, q):
                    half, o = k // 6, k % 6 * S
                    dve.tensor_tensor(
                        inp[:, :, 1:].rearrange("p (c n) e -> p c n e", c=KE * B),
                        uc[half][:, :, o:o + S].unsqueeze(2).broadcast_to([P, KE * B, N, S]),
                        bc[q][:, 0].unsqueeze(1).broadcast_to([P, KE, B * N, S]),
                        ALU.mult).then_inc(inp_ready, 1)

                def scan(k, q, j):
                    dve.wait_ge(norm_ready, j + 1)
                    dve.tensor_tensor(rows(inp[:])[:, :, :, :, 0], rows(h[:])[:, :, :, :, S],
                                      rc[:].unsqueeze(1).unsqueeze(3).broadcast_to([P, KE, B, N]),
                                      ALU.mult).then_inc(carry_ready, 1)
                    dve.wait_ge(carry_ready, FIRST + j + 1)
                    dve.tensor_tensor_scan(h[:].rearrange("p r e -> p (r e)"),
                                           decay[:, q, k, :], inp[:].rearrange("p r e -> p (r e)"),
                                           0.0, ALU.mult, ALU.add).then_inc(h_ready, 1)

                copy_sum(0)
                dve.wait_ge(u_in[0], 16)
                dve.wait_ge(bc_in[0], 16)
                inputs(0, 0)

                def turn(t, slots):
                    for s in range(slots):
                        j, c, cs, q = t * BODY + s, t * 2 + s // CB, s % CB, s // CB
                        last = slots == TAIL and s == slots - 1
                        scan(cs, q, j)
                        dve.wait_ge(h_ready, j + 2)
                        pl = s // 2
                        if s % 2 == 0:
                            dve.wait_ge(y_summed, t * PAIRS_BODY + pl + 1)
                        dve.tensor_tensor(
                            hc[:, pl % 2, :, s % 2 * S:(s % 2 + 1) * S].rearrange("p (c r) e -> p c r e", c=KE),
                            h[:, :, 0:S].rearrange("p (c r) e -> p c r e", c=KE),
                            bc[s % 3][:, 1].unsqueeze(1).broadcast_to([P, KE, B * N, S]),
                            ALU.mult).then_inc(hc_ready, 1)
                        if last:
                            continue
                        copy_sum(j + 1)
                        k = (cs + 1) % CB
                        if k == 0:
                            dve.wait_ge(u_in[0], c * 16 + 32)
                        if k == 6:
                            dve.wait_ge(u_in[1], c * 16 + 16)
                        r, turns = (s + 1) % 3, t * 8 + (s + 1) // 3 + 1
                        dve.wait_ge(bc_in[r], turns * 16)
                        inputs(k, r)
                with dve.Fori(0, TURNS) as t:
                    turn(t, BODY)
                turn(TURNS, TAIL)


def post_stage(nc, dram, out):
    with ExitStack() as ctx:
        def sb(name, shape):
            return ctx.enter_context(nc.sbuf_tensor(name, shape, F32))

        def sem(name):
            return ctx.enter_context(nc.semaphore(name))

        psT = ctx.enter_context(nc.psum_tensor("q_psT", [P, KD, COLS], F32))
        psM = ctx.enter_context(nc.psum_tensor("q_psM", [P, 2, COLS], F32))
        psX = ctx.enter_context(nc.psum_tensor("q_psX", [P, G, D], F32))
        psO = ctx.enter_context(nc.psum_tensor("q_psO", [P, G, D], F32))
        w = FfnWeights(nc, ctx, dram, "fb")
        ffn = Ffn(nc, ctx, "fb", w, psT, psM, psO)
        wout = sb("wout", [P, KE, D])
        dpar = sb("dpar", [P, KE])
        rscale = sb("rscale", [P, 1])
        ys = sb("ys", [P, KE, COLS])
        xc = sb("q_xc", [P, KE, COLS])
        sg = sb("q_sg", [P, KE, COLS])
        r = sb("q_r", [P, G, D])
        x2 = sb("x2", [P, G, D])
        res = sb("res", [P, G, D])
        w1n = sb("q_w1n", [P, KH, D])
        w2abs = sb("q_w2abs", [P, KH, D])
        q_loaded = sem("q_loaded")
        scale_steps = sem("scale_steps")
        y_in, xc_in, sg_in, r_in = (sem(n) for n in ("q_y_in", "q_xc_in", "q_sg_in", "q_r_in"))
        skip_added = sem("skip_added")
        gated = sem("gated")
        out_done = sem("out_done")
        x2_ready = sem("x2_ready")
        stored = sem("stored")
        prime(nc, ffn.primed() + [skip_added, gated, out_done, x2_ready, stored])

        def steps(i):
            return bass.ds(i * TT, TT)

        with nc.Block() as block:
            @block.sync
            def _(sp):
                sp.dma_start(wout[:], dram["woutT"].rearrange("(k p) m -> p k m", p=P)).then_inc(q_loaded, 16)
                sp.dma_start(dpar[:], dram["dpar"]).then_inc(q_loaded, 16)
                sp.dma_start(rscale[:], dram["rscale"].broadcast_to([P, 1])).then_inc(q_loaded, 16)
                def load(name, tile, done, i):
                    sp.dma_start(tile[:].rearrange("p a (b t) -> p (a b) t", b=B),
                                 dram[name][:, :, steps(i)]).then_inc(done, 16)

                def fetch(i):
                    hold(sp, (w.loaded, 48), skip_added, FIRST + i * KE)
                    load("xc", xc, xc_in, i)
                    hold(sp, (w.loaded, 48), gated, FIRST + i)
                    load("sg", sg, sg_in, i)
                    hold(sp, (w.loaded, 48), out_done, FIRST + i)
                    load("y", ys, y_in, i)
                    hold(sp, (w.loaded, 48), x2_ready, FIRST + i)
                    for b in range(B):
                        sp.dma_start(r[:, 2 * b:2 * b + 2, :],
                                     dram["r"][b, steps(i), :].rearrange("(h p) d -> p h d", p=P)).then_inc(r_in, 16)

                def store(i):
                    hold(sp, (w.loaded, 48), ffn.dst_ready, FIRST + i + 1)
                    for b in range(B):
                        sp.dma_start(out[b, steps(i), :].rearrange("(h p) d -> p h d", p=P),
                                     res[:, 2 * b:2 * b + 2, :]).then_inc(stored, 16)

                fetch(0)
                w.load(sp, w1n)
                fetch(1)
                with sp.Fori(0, TILES - 2) as i:
                    fetch(i + 2)
                    store(i)
                store(TILES - 2)
                store(TILES - 1)
                sp.wait_ge(stored, FIRST + 32 * TILES)

            @block.gpsimd
            def _(pool):
                w.on_pool(pool)
                with pool.Fori(0, TILES) as i:
                    ffn.norm.on_pool(pool, i)

            @block.tensor
            def _(pe):
                pe.wait_ge(q_loaded, 48)

                def project(i):
                    pe.wait_ge(gated, FIRST + i + 1)
                    pe.wait_ge(x2_ready, FIRST + i)
                    for g in range(G):
                        for k in range(KE):
                            mm = pe.matmul(psX[:, g, :], ys[:, k, g * P:(g + 1) * P], wout[:, k, :],
                                           start=(k == 0), stop=(k == KE - 1))
                    mm.then_inc(out_done, 1)

                def body(i, ahead):
                    ffn.pe_in(pe, i)
                    ffn.pe_up(pe, i)
                    if ahead:
                        project(i + 1)
                    ffn.pe_down(pe, i)

                project(0)
                w.on_pe(pe, w2abs, psO[:, 0, :])
                pe.wait_ge(w.signs, 2)
                pe.wait_ge(w.ready, 3)
                with pe.Fori(0, TILES - 1) as i:
                    body(i, True)
                body(TILES - 1, False)

            @block.scalar
            def _(act):
                act.wait_ge(q_loaded, 48)
                act.activation(rscale[:], rscale[:], ACT.Exp, scale=-1.0).then_inc(scale_steps, 1)
                w.on_act(act, w1n, w2abs)
                act.wait_ge(w.ready, 3)
                with act.Fori(0, TILES) as i:
                    ffn.act_in(act, i)
                    ffn.act_up(act, i)

            @block.vector
            def _(dve):
                dve.wait_ge(q_loaded, 48)
                dve.wait_ge(scale_steps, 1)
                dve.tensor_scalar(rscale[:], rscale[:], 1.0, None, ALU.add).then_inc(scale_steps, 1)
                dve.wait_ge(scale_steps, 2)
                dve.reciprocal(rscale[:], rscale[:]).then_inc(scale_steps, 1)
                dve.wait_ge(scale_steps, 3)
                dve.tensor_scalar(rscale[:], rscale[:], 0.5, None, ALU.mult).then_inc(scale_steps, 1)
                dve.wait_ge(scale_steps, 4)

                def gate(i):
                    dve.wait_ge(y_in, i * 16 + 16)
                    dve.wait_ge(xc_in, i * 16 + 16)
                    dve.wait_ge(sg_in, i * 16 + 16)
                    for k in range(KE):
                        dve.scalar_tensor_tensor(out=ys[:, k, :], in0=xc[:, k, :], scalar=dpar[:, k:k + 1],
                                                 in1=ys[:, k, :], op0=ALU.mult, op1=ALU.add).then_inc(skip_added, 1)
                    dve.wait_ge(skip_added, FIRST + i * KE + KE)
                    dve.tensor_tensor(ys[:], ys[:], sg[:], ALU.mult).then_inc(gated, 1)

                def residual(i):
                    dve.wait_ge(out_done, FIRST + i + 1)
                    dve.wait_ge(r_in, i * 32 + 32)
                    dve.wait_ge(ffn.kept, FIRST + i)
                    dve.scalar_tensor_tensor(out=x2[:], in0=psX[:], scalar=rscale[:], in1=r[:], op0=ALU.mult,
                                             op1=ALU.add).then_inc(x2_ready, 1)
                    dve.wait_ge(x2_ready, FIRST + i + 1)
                    ffn.dve_in(dve, x2, i)

                def body(i, ahead):
                    if ahead:
                        gate(i + 1)
                        residual(i + 1)
                    dve.wait_ge(stored, FIRST + i * 32)
                    ffn.dve_out(dve, res, i)
                    if ahead:
                        dve.wait_ge(ffn.dst_ready, FIRST + i + 1)
                        ffn.dve_keep(dve, x2, i + 1)

                gate(0)
                residual(0)
                w.on_dve(dve, psO[:, 0, :])
                ffn.dve_keep(dve, x2, 0)
                with dve.Fori(0, TILES - 1) as i:
                    body(i, True)
                body(TILES - 1, False)


def build(nc, dram, out):
    def scratch(name, shape):
        return nc.dram_tensor(f"scratch_{name}", shape, F32, kind="Internal").ap()

    dram = dict(dram)
    dram["dt"] = scratch("dt", (P, KE * B, LP))
    dram["u"] = scratch("u", (P, KE * B, LP))
    dram["xc"] = scratch("xc", (P, KE * B, L))
    dram["sg"] = scratch("sg", (P, KE * B, L))
    dram["y"] = scratch("y", (P, KE * B, LP))
    dram["bc"] = scratch("bc", (2 * N, B, LP))
    dram["blk"] = scratch("blk", (CHUNKS * CB, 2, B, N, S))
    dram["r"] = scratch("r", (B, L, D))
    pre_stage(nc, dram)
    scan_stage(nc, dram)
    post_stage(nc, dram, out)


def kernel(L0_attn_x, L0_attn_norm_w, L0_attn_W_in, L0_attn_conv_w, L0_attn_conv_b, L0_attn_W_dt, L0_attn_b_dt,
           L0_attn_W_B, L0_attn_W_C, L0_attn_A_log, L0_attn_D_param, L0_attn_W_out, L0_attn_residual_scale,
           L0_ffn_w1, L0_ffn_b1, L0_ffn_w2, L0_ffn_b2):
    import numpy as np
    import concourse.bacc as bacc
    from concourse.bass_utils import run_bass_kernel_spmd

    def a(x):
        return np.asarray(x)

    def cols(x, k):
        x = a(x).reshape(k, P, -1)
        return x.transpose(1, 0, 2).reshape(P, -1)

    ins = {
        "x": a(L0_attn_x), "normw": cols(L0_attn_norm_w, KD), "winT": a(L0_attn_W_in).T,
        "convw": cols(a(L0_attn_conv_w).reshape(E, TAPS), KE).reshape(P, KE, TAPS), "convb": cols(L0_attn_conv_b, KE),
        "wdtT": a(L0_attn_W_dt).T, "bdt": cols(L0_attn_b_dt, KE),
        "wbcT": np.concatenate([a(L0_attn_W_B), a(L0_attn_W_C)], 0).T,
        "alog": cols(L0_attn_A_log, KE), "dpar": cols(L0_attn_D_param, KE), "woutT": a(L0_attn_W_out).T,
        "rscale": a(L0_attn_residual_scale).reshape(1, 1),
        "w1": a(L0_ffn_w1), "w1T": a(L0_ffn_w1).T, "b1": cols(L0_ffn_b1, KH),
        "w2T": a(L0_ffn_w2).T, "b2": a(L0_ffn_b2).reshape(1, D),
    }
    nc = bacc.Bacc("TRN2", target_bir_lowering=False, num_devices=1)
    arrays, dram = {}, {}
    for name, x in ins.items():
        x = np.ascontiguousarray(x)
        arrays[f"in_{name}"] = x
        dram[name] = nc.dram_tensor(f"in_{name}", x.shape, mybir.dt.from_np(x.dtype), kind="ExternalInput").ap()
    out = nc.dram_tensor("out_y", (B, L, D), F32, kind="ExternalOutput").ap()
    build(nc, dram, out)
    got = run_bass_kernel_spmd(nc, [arrays], core_ids=[0])
    return got.results[0]["out_y"]
```
